# Optimizing a Trainium2 kernel written in Bass

```python
import numpy as np
import jax
import jax.numpy as jnp

def _softmax(x, axis=-1):
    return jax.nn.softmax(x, axis=axis)

def _gelu(x):
    return jax.nn.gelu(x, approximate=True)

def _silu(x):
    return jax.nn.silu(x)

def _sigmoid(x):
    return jax.nn.sigmoid(x)

def _layernorm(x, axis=-1, eps=1e-05):
    m = jnp.mean(x, axis=axis, keepdims=True)
    v = jnp.var(x, axis=axis, keepdims=True)
    return (x - m) / jnp.sqrt(v + eps)

def _scatter_add(tgt, idx, src, axis=0):
    return tgt.at[idx].add(src)

def _segment_sum(src, seg, n):
    return jax.ops.segment_sum(src, seg, n)
kernel_name = 'mk_gnn_preln_d2_gnn_r32_fff169'

def setup_inputs(seed: int=0):
    np.random.seed(seed)
    _w = jnp.asarray

    def _rec_inputs():
        import jax
        import jax.numpy as jnp
        _gk = jax.random.key(seed)
        x = -0.0002117 + 1 * jax.random.normal(jax.random.fold_in(_gk, 1), (50000, 256), jnp.float32)
        src = jax.random.randint(jax.random.fold_in(_gk, 2), (25000,), 0, 50000, jnp.int32)
        dst = jax.random.randint(jax.random.fold_in(_gk, 3), (25000,), 0, 50000, jnp.int32)
        _o = jnp.argsort(dst, stable=True)
        src = src[_o]
        dst = dst[_o]
        edge_type_8 = jax.random.randint(jax.random.fold_in(_gk, 13), (25000,), 0, 8, jnp.int32)
        return (x, src, dst, edge_type_8)
    x, src, dst, edge_type_8 = _rec_inputs()

    def _L0_gnn_setup():
        import jax, jax.numpy as jnp
        import numpy as np
        N_NODES = 3125
        N_EDGES = 10000
        DIM = 256
        BN_EPS = 1e-05
        key = jax.random.key(seed)
        k1, k2, k3 = jax.random.split(key, 3)
        x = jax.random.normal(k1, (N_NODES, DIM), dtype=jnp.float32)
        W = jax.random.normal(k2, (DIM, DIM), dtype=jnp.float32) * (1.0 / np.sqrt(DIM))
        b = jnp.zeros((DIM,), dtype=jnp.float32)
        gamma = jnp.ones((DIM,), dtype=jnp.float32)
        beta = jnp.zeros((DIM,), dtype=jnp.float32)
        edge_index = jax.random.randint(k3, (2, N_EDGES), 0, N_NODES, dtype=jnp.int64)
        return {'x': x, 'W': W, 'b': b, 'gamma': gamma, 'beta': beta, 'edge_index': edge_index}
    _L0_gnn_all = _L0_gnn_setup()
    _L0_gnn_in = {k: v for k, v in _L0_gnn_all.items() if k in ('W', 'b', 'gamma', 'beta')}
    del _L0_gnn_all

    def _L1_gnn_setup():
        import jax, jax.numpy as jnp
        import numpy as np
        N_NODES = 625
        N_EDGES = 10000
        NUM_RELS = 8
        DIM = 256
        BN_EPS = 1e-05
        key = jax.random.key(seed)
        k1, k2, k3, k4, k5 = jax.random.split(key, 5)
        h = jax.random.normal(k1, (N_NODES, DIM), dtype=jnp.float32)
        weight = jax.random.normal(k2, (NUM_RELS, DIM, DIM), dtype=jnp.float32) * 0.05
        gamma = jnp.ones((DIM,), dtype=jnp.float32)
        beta = jnp.zeros((DIM,), dtype=jnp.float32)
        src = jax.random.randint(k3, (N_EDGES,), 0, N_NODES, dtype=jnp.int32)
        dst = jax.random.randint(k4, (N_EDGES,), 0, N_NODES, dtype=jnp.int32)
        rel = jax.random.randint(k5, (N_EDGES,), 0, NUM_RELS, dtype=jnp.int32)
        return {'h': h, 'weight': weight, 'gamma': gamma, 'beta': beta, 'src': src, 'dst': dst, 'rel': rel}
    _L1_gnn_all = _L1_gnn_setup()
    _L1_gnn_in = {k: v for k, v in _L1_gnn_all.items() if k in ('weight', 'gamma', 'beta')}
    del _L1_gnn_all
    return {'x': x, 'src': src, 'dst': dst, 'edge_type_8': edge_type_8, 'L0_gnn_W': _L0_gnn_in['W'], 'L0_gnn_b': _L0_gnn_in['b'], 'L0_gnn_gamma': _L0_gnn_in['gamma'], 'L0_gnn_beta': _L0_gnn_in['beta'], 'L1_gnn_weight': _L1_gnn_in['weight'], 'L1_gnn_gamma': _L1_gnn_in['gamma'], 'L1_gnn_beta': _L1_gnn_in['beta']}

def reference(x, src, dst, edge_type_8, L0_gnn_W, L0_gnn_b, L0_gnn_gamma, L0_gnn_beta, L1_gnn_weight, L1_gnn_gamma, L1_gnn_beta):
    import jax
    import jax.numpy as jnp

    def _L0_gnn_ref(x, W, b, gamma, beta, edge_index):
        import jax, jax.numpy as jnp
        import numpy as np
        N_NODES = 3125
        N_EDGES = 10000
        DIM = 256
        BN_EPS = 1e-05
        N = x.shape[0]
        loop = jnp.arange(N, dtype=edge_index.dtype)
        row = jnp.concatenate([edge_index[0], loop])
        col = jnp.concatenate([edge_index[1], loop])
        deg = jax.ops.segment_sum(jnp.ones_like(col, dtype=x.dtype), col, num_segments=N)
        dinv = jax.lax.rsqrt(deg)
        norm = dinv[row] * dinv[col]
        h = x @ W
        msg = h[row] * norm[:, None]
        out = jax.ops.segment_sum(msg, col, num_segments=N) + b
        mean = jnp.mean(out, axis=0)
        var = jnp.var(out, axis=0)
        out = (out - mean) * jax.lax.rsqrt(var + BN_EPS) * gamma + beta
        return jnp.tanh(out)

    def _L1_gnn_ref(h, weight, gamma, beta, src, dst, rel):
        import jax, jax.numpy as jnp
        import numpy as np
        N_NODES = 625
        N_EDGES = 10000
        NUM_RELS = 8
        DIM = 256
        BN_EPS = 1e-05
        all_h = jnp.einsum('ni,rio->nro', h, weight)
        msg = all_h[src, rel]
        agg = jax.ops.segment_sum(msg, dst, num_segments=h.shape[0])
        mean = jnp.mean(agg, axis=0)
        var = jnp.mean(jnp.square(agg - mean), axis=0)
        out = (agg - mean) * jax.lax.rsqrt(var + BN_EPS) * gamma + beta
        return out
    edge_index = jnp.stack([src, dst])
    h = jnp.maximum(_layernorm(x, axis=-1), 0.0)
    x = x + _L0_gnn_ref(h, L0_gnn_W, L0_gnn_b, L0_gnn_gamma, L0_gnn_beta, edge_index)
    h = jnp.maximum(_layernorm(x, axis=-1), 0.0)
    x = x + _L1_gnn_ref(h, L1_gnn_weight, L1_gnn_gamma, L1_gnn_beta, src, dst, edge_type_8)
    return x

_drawn_inputs = setup_inputs


def setup_inputs(seed=0):
    import zlib

    import numpy as np

    out = dict(_drawn_inputs(seed))
    spreads = {'L0_gnn_b': (0.0, 0.1),
     'L0_gnn_gamma': (1.0, 0.2),
     'L0_gnn_beta': (0.0, 0.1),
     'L1_gnn_gamma': (1.0, 0.2),
     'L1_gnn_beta': (0.0, 0.1)}
    factors = {}
    for name, (base, spread) in spreads.items():
        noise = np.random.default_rng([zlib.crc32(name.encode()), seed]).standard_normal(out[name].shape)
        drawn = base * np.exp(spread * noise) if base else spread * noise
        out[name] = jnp.asarray(drawn.astype(out[name].dtype))
    for name, factor in factors.items():
        out[name] = (out[name] * factor).astype(out[name].dtype)
    return out
```

```python
from contextlib import ExitStack

import concourse.bass as bass
from concourse import mybir

F32 = mybir.dt.float32
BF16 = mybir.dt.bfloat16
I32 = mybir.dt.int32
ALU = mybir.AluOpType
ACT = mybir.ActivationFunctionType

P = 128
J = 5
RELS = 8
EPS = 1e-5
NOWHERE = 1.0e6


class Plan:

    def __init__(self, rows):
        self.rows = rows
        self.full_tiles, self.tail = divmod(rows, P)
        assert self.full_tiles % J == 0
        self.full_groups = self.full_tiles // J
        self.groups = self.full_groups + (self.tail > 0)
        self.tiles = self.full_tiles + (self.tail > 0)


class Group:

    def __init__(self, plan, loop, r):
        self.plan, self.loop, self.r = plan, loop, r
        static = isinstance(loop, int)
        self.number = 2 * loop + r
        self.half = loop + r // 2
        self.par = r % 2
        self.exists = not static or 0 <= r < plan.groups
        short = static and r == plan.full_groups
        self.tiles = 1 if short else J
        self.n = plan.tail if short else P

    def at(self, d):
        return Group(self.plan, self.loop, self.r + d)

    def rows(self, dram):
        count = self.tiles * self.n
        if isinstance(self.number, int):
            part = dram[self.number * J * P:self.number * J * P + count, :]
        else:
            part = dram[bass.ds(self.number * (J * P), count), :]
        return part.rearrange("(j p) d -> p j d", p=self.n)

    def cols(self, table, n=None):
        n = self.n if n is None else n
        if isinstance(self.number, int):
            return table[0:n, self.number * J:self.number * J + self.tiles]
        return table[0:n, bass.ds(self.number * J, self.tiles)]

    def col(self, table, j):
        if isinstance(self.number, int):
            return table[0:self.n, self.number * J + j:self.number * J + j + 1]
        return table[0:self.n, bass.ds(self.number * J + j, 1)]

    def tile(self, j):
        return self.number * J + (j + 1)

    def loads(self, each=1):
        return self.half * (16 * J * each) + 16 * self.tiles * each


def sweep(eng, plan, start, lo, hi, end, step):
    pairs = max(0, (hi - lo) // 2)
    for r in range(start, lo if pairs else end):
        step(Group(plan, 0, r))
    if pairs:
        with eng.Fori(0, pairs) as i:
            for u in range(2):
                step(Group(plan, i, lo + u))
        for r in range(lo + 2 * pairs, end):
            step(Group(plan, 0, r))


def wait(eng, sem, value):
    if isinstance(value, int) and value <= 0:
        return
    eng.wait_ge(sem, value)


class Ctx:

    def __init__(self, nc, name):
        self.nc, self.name, self.stack = nc, name, ExitStack()

    def __enter__(self):
        self.stack.__enter__()
        return self

    def __exit__(self, *a):
        return self.stack.__exit__(*a)

    def sb(self, name, shape, dt=F32):
        return self.stack.enter_context(self.nc.sbuf_tensor(f"{self.name}_{name}", shape, dt))

    def ps(self, name, shape):
        return self.stack.enter_context(self.nc.psum_tensor(f"{self.name}_{name}", shape, F32))

    def sem(self, name):
        return self.stack.enter_context(self.nc.semaphore(f"{self.name}_{name}"))

    def sems(self, name):
        return [self.sem(f"{name}{k}") for k in range(2)]

    def block(self):
        return self.stack.enter_context(self.nc.Block())


class Chain:

    def __init__(self, eng, sem):
        self.eng, self.sem, self.n = eng, sem, 0

    def __call__(self, ins):
        self.n += 1
        ins.then_inc(self.sem, 1)
        self.eng.wait_ge(self.sem, self.n)


def gather(pool, out, table, index, limit):
    return pool.indirect_dma_start(
        out=out, out_offset=None, in_=table[:, :],
        in_offset=bass.IndirectOffsetOnAxis(ap=index, axis=0), bounds_check=limit, oob_is_err=False)


def edge_tables(nc, k, src, dst, rel):
    E, ET, BT = k.E, k.edges.tiles, k.slots.tiles
    with Ctx(nc, "et") as c:
        chunks = -(-ET // P)
        raw = c.sb("raw", [P, 4, chunks, P], I32)
        rawf = c.sb("rawf", [P, 4, chunks, P])
        relf = c.sb("relf", [P, ET])
        dsti = c.sb("dsti", [P, 2, ET], I32)
        mask = c.sb("mask", [P, RELS, ET])
        run = c.sb("run", [P, RELS, ET])
        zeros = c.sb("zeros", [P, ET])
        total = c.sb("total", [P, RELS])
        before = c.sb("before", [P, 2 * RELS])
        tiles_i = c.sb("tiles_i", [P, 2, RELS], I32)
        tiles_f = c.sb("tiles_f", [P, RELS])
        tile_end = c.sb("tile_end", [P, RELS])
        base = c.sb("base", [P, RELS])
        slot = c.sb("slot", [P, ET])
        slot_p = c.sb("slot_p", [P, 3, ET], I32)
        tile_rel = c.sb("tile_rel", [P, BT])
        ps = c.ps("ps", [P, 4 * chunks, P])
        ps_count = c.ps("ps_count", [P, 512])
        s_pad, s_rows, s_const = c.sem("padded"), c.sem("rows"), c.sem("constants")
        s_rowf, s_turned, s_own = c.sem("row_floats"), c.sem("turned"), c.sem("own")
        s_total, s_before, s_zero = c.sem("totals"), c.sem("before_sem"), c.sem("zero_slots")
        s_slots, s_scatter, s_back = c.sem("slots"), c.sem("scattered"), c.sem("read_back")
        s_own_act = c.sem("own_act")
        block = c.block()
        lists = [(src, 0, E), (dst, 0, E), (dst, 1, E - 1), (rel, 0, E)]
        loads = sum((n // P > 0) + (n // P > P) + (n % P > 0) for _, _, n in lists)

        @block.sync
        def _(sp):
            for dram, there in k.const_loads:
                sp.dma_start(there, dram).then_inc(s_const, 16)
            sp.wait_ge(s_pad, 4)
            for kind, (a, first, n) in enumerate(lists):
                full, rest = divmod(n, P)
                for ch in range(chunks):
                    rows = min(full - ch * P, P)
                    if rows > 0:
                        at = first + ch * P * P
                        sp.dma_start(raw[0:rows, kind, ch, :],
                                     a[at:at + rows * P].rearrange("(r i) -> r i", i=P)).then_inc(s_rows, 16)
                if rest:
                    at = first + full * P
                    sp.dma_start(raw[full % P:full % P + 1, kind, full // P, 0:rest],
                                 a[at:at + rest].rearrange("(r i) -> r i", r=1)).then_inc(s_rows, 16)
            sp.wait_ge(s_zero, 1)
            sp.dma_start(k.slot_src_dram.rearrange("(p t) o -> p (t o)", p=P), k.slot_src[:, :]).then_inc(s_back, 16)
            sp.wait_ge(s_back, 16)
            sp.wait_ge(s_scatter, 16 * ET)
            sp.dma_start(k.slot_src[:, :], k.slot_src_dram.rearrange("(p t) o -> p (t o)", p=P)).then_inc(s_back, 16)
            sp.wait_ge(s_back, 32)
            sp.wait_ge(s_const, 16 * len(k.const_loads))

        @block.gpsimd
        def _(pool):
            for kind, fill in enumerate((0, k.N, k.N, RELS)):
                pool.memset(raw[:, kind, :, :], fill).then_inc(s_pad, 1)
            pool.memset(k.slot_src[:, :], 0).then_inc(s_zero, 1)
            last_slot = pool.to_reg(P * BT - 1)
            pool.wait_ge(s_back, 16)
            pool.wait_ge(s_slots, 1)
            for t in range(ET):
                pool.indirect_dma_start(
                    out=k.slot_src_dram[:, :],
                    out_offset=bass.IndirectOffsetOnAxis(ap=slot_p[:, 2, t:t + 1], axis=0),
                    in_=k.src_i[:, t:t + 1], in_offset=None, bounds_check=last_slot,
                    oob_is_err=False).then_inc(s_scatter, 16)

        @block.vector
        def _(dve):
            own = Chain(dve, s_own)
            own(nc.vector.memset(zeros[:, :], 0.0))
            dve.wait_ge(s_rows, 16 * loads)
            own(nc.vector.tensor_copy(rawf[:, :, :, :], raw[:, :, :, :]))
            nc.vector.tensor_tensor(rawf[:, 2, :, :], rawf[:, 1, :, :], rawf[:, 2, :, :],
                                    ALU.not_equal).then_inc(s_rowf, 1)
            dve.wait_ge(s_turned, 1)
            for kind, out in ((0, k.src_f), (1, k.dst_f), (2, k.last_f), (3, relf)):
                for ch in range(chunks):
                    w = min(ET - ch * P, P)
                    own(nc.vector.tensor_copy(out[:, ch * P:ch * P + w], ps[:, kind * chunks + ch, 0:w]))
            own(nc.vector.tensor_copy(k.src_i[:, :], k.src_f[:, :]))
            own(nc.vector.tensor_copy(dsti[:, 0, :], k.dst_f[:, :]))
            own(nc.vector.tensor_scalar(dsti[:, 1, :], dsti[:, 0, :], 7, None, ALU.arith_shift_right))
            own(nc.vector.tensor_copy(k.dst_high[:, :], dsti[:, 1, :]))
            own(nc.vector.tensor_scalar(dsti[:, 1, :], dsti[:, 0, :], P - 1, None, ALU.bitwise_and))
            own(nc.vector.tensor_copy(k.dst_low[:, :], dsti[:, 1, :]))
            dve.wait_ge(s_const, 16 * len(k.const_loads))
            own(nc.vector.memset(k.dst_before[:, 0:1], -1.0))
            own(nc.vector.tensor_scalar(k.dst_before[:, 1:ET], k.dst_f[:, 0:ET - 1], k.is_last[:, 0:1],
                                        k.is_last[:, 1:2], ALU.mult, ALU.add))
            for r in range(RELS):
                own(nc.vector.tensor_scalar(mask[:, r, :], relf[:, :], float(r), None, ALU.is_equal))
                own(nc.vector.tensor_tensor_scan(run[:, r, :], mask[:, r, :], zeros[:, :], 0.0, ALU.add, ALU.add))
            nc.vector.tensor_copy(total[:, :], run[:, :, ET - 1]).then_inc(s_total, 1)
            dve.wait_ge(s_before, 1)
            own(nc.vector.tensor_copy(before[:, :], ps_count[:, 0:2 * RELS]))
            own(nc.vector.tensor_scalar(tiles_f[:, :], before[:, RELS:2 * RELS], float(P - 1), None, ALU.add))
            own(nc.vector.tensor_copy(tiles_i[:, 0, :], tiles_f[:, :]))
            own(nc.vector.tensor_scalar(tiles_i[:, 1, :], tiles_i[:, 0, :], 7, None, ALU.arith_shift_right))
            own(nc.vector.tensor_copy(tiles_f[:, :], tiles_i[:, 1, :]))
            own(nc.vector.tensor_tensor_scan(tile_end[:, :], tiles_f[:, :], zeros[:, 0:RELS], 0.0, ALU.add, ALU.add))
            own(nc.vector.tensor_tensor(tiles_f[:, :], tile_end[:, :], tiles_f[:, :], ALU.subtract))
            own(nc.vector.scalar_tensor_tensor(base[:, :], tiles_f[:, :], float(P), before[:, 0:RELS],
                                               ALU.mult, ALU.add))
            own(nc.vector.tensor_scalar(base[:, :], base[:, :], 1.0, None, ALU.subtract))
            own(nc.vector.tensor_scalar(slot[:, :], relf[:, :], float(RELS), NOWHERE, ALU.is_equal, ALU.mult))
            for r in range(RELS):
                own(nc.vector.scalar_tensor_tensor(run[:, r, :], run[:, r, :], base[:, r:r + 1], mask[:, r, :],
                                                   ALU.add, ALU.mult))
                own(nc.vector.tensor_tensor(slot[:, :], slot[:, :], run[:, r, :], ALU.add))
            own(nc.vector.tensor_copy(k.slot_i[:, :], slot[:, :]))
            own(nc.vector.tensor_scalar(slot_p[:, 0, :], k.slot_i[:, :], P - 1, None, ALU.bitwise_and))
            own(nc.vector.tensor_scalar(slot_p[:, 1, :], k.slot_i[:, :], 7, None, ALU.arith_shift_right))
            own(nc.vector.tensor_copy(mask[:, 0, :], slot_p[:, 0, :]))
            own(nc.vector.tensor_copy(mask[:, 1, :], slot_p[:, 1, :]))
            own(nc.vector.scalar_tensor_tensor(mask[:, 2, :], mask[:, 0, :], float(BT), mask[:, 1, :],
                                               ALU.mult, ALU.add))
            own(nc.vector.tensor_scalar(mask[:, 3, :], slot[:, :], NOWHERE, NOWHERE, ALU.is_ge, ALU.mult))
            own(nc.vector.tensor_tensor(mask[:, 2, :], mask[:, 2, :], mask[:, 3, :], ALU.add))
            nc.vector.tensor_copy(slot_p[:, 2, :], mask[:, 2, :]).then_inc(s_slots, 1)
            own(nc.vector.memset(tile_rel[:, :], 0.0))
            for r in range(RELS - 1):
                own(nc.vector.scalar_tensor_tensor(tile_rel[:, :], k.iota[:, 0:BT], tile_end[:, r:r + 1],
                                                   tile_rel[:, :], ALU.is_ge, ALU.add))
            own(nc.vector.tensor_scalar(tile_rel[:, :], tile_rel[:, :], float(k.D), None, ALU.mult))
            own(nc.vector.tensor_copy(k.tile_weight[:, :], tile_rel[:, :]))

        @block.tensor
        def _(pe):
            pe.wait_ge(s_rowf, 1)
            pe.wait_ge(s_const, 16 * len(k.const_loads))
            for kind in range(4):
                for ch in range(chunks):
                    w = min(ET - ch * P, P)
                    last = nc.tensor.transpose(ps[:, kind * chunks + ch, 0:w], rawf[0:w, kind, ch, :],
                                               k.ident[0:w, 0:w])
            last.then_inc(s_turned, 1)
            pe.wait_ge(s_total, 1)
            nc.tensor.matmul(ps_count[:, 0:RELS], k.below[:, :], total[:, :], start=True, stop=True)
            nc.tensor.matmul(ps_count[:, RELS:2 * RELS], k.ones[:, :], total[:, :], start=True,
                             stop=True).then_inc(s_before, 1)


def degree_tables(nc, k):
    ET, NT = k.edges.tiles, k.node_cols
    with Ctx(nc, "dt") as c:
        hot_low = c.sb("hot_low", [P, 2, P], BF16)
        hot_high = c.sb("hot_high", [P, 2, NT], BF16)
        hist = c.sb("hist", [P, NT])
        zeros = c.sb("zeros", [P, NT])
        scan = c.sb("scan", [P, NT])
        tmp = c.sb("tmp", [P, 2, NT])
        turned = c.sb("turned", [P, -(-NT // P), P])
        ps_hist = c.ps("ps_hist", [P, 512])
        ps_sum = c.ps("ps_sum", [P, 2, 512])
        ps_turn = c.ps("ps_turn", [P, 4, P])
        s_hot, s_counted, s_own = c.sem("hot"), c.sem("counted"), c.sem("own")
        s_hist, s_sums, s_deg, s_root = c.sem("hist_sem"), c.sem("sums"), c.sem("deg"), c.sem("root")
        s_dinv, s_turn, s_copied, s_out = c.sem("dinv"), c.sem("turn"), c.sem("copied"), c.sem("out")
        block = c.block()
        pairs = (ET - 2) // 2

        def each_tile(eng, step):
            step(0, 0)
            with eng.Fori(0, pairs) as i:
                for u in range(2):
                    step(2 * i + 1 + u, (1 + u) % 2)
            for t in range(1 + 2 * pairs, ET):
                step(t, t % 2)

        def column(table, t):
            return table[:, t:t + 1] if isinstance(t, int) else table[:, bass.ds(t, 1)]

        @block.vector
        def _(dve):
            def step(t, b):
                wait(dve, s_counted, t - 1)
                nc.vector.tensor_scalar(hot_low[:, b, :], k.iota[:, 0:P], column(k.dst_low, t), None, ALU.is_equal)
                nc.vector.tensor_scalar(hot_high[:, b, :], k.iota[:, 0:NT], column(k.dst_high, t), None,
                                        ALU.is_equal).then_inc(s_hot, 1)

            step(0, 0)
            step(1, 1)
            with dve.Fori(0, (ET - 2) // 2) as i:
                for u in range(2):
                    step(2 * i + 2 + u, u)
            for t in range(2 + 2 * ((ET - 2) // 2), ET):
                step(t, t % 2)
            own = Chain(dve, s_own)
            own(nc.vector.memset(zeros[:, :], 0.0))
            dve.wait_ge(s_counted, ET)
            own(nc.vector.tensor_copy(hist[:, :], ps_hist[:, 0:NT]))
            own(nc.vector.tensor_scalar(tmp[:, 0, :], hist[:, :], 1.0, None, ALU.add))
            nc.vector.tensor_scalar(k.has_edge[:, :], hist[:, :], 0.5, None, ALU.is_gt).then_inc(s_hist, 1)
            dve.wait_ge(s_root, 1)
            nc.vector.reciprocal(k.dinv[:, :], tmp[:, 1, :]).then_inc(s_dinv, 1)
            dve.wait_ge(s_sums, 1)
            own(nc.vector.tensor_copy(tmp[:, 0, :], ps_sum[:, 0, 0:NT]))
            own(nc.vector.tensor_tensor_scan(scan[:, :], tmp[:, 0, :], zeros[:, :], 0.0, ALU.add, ALU.add))
            own(nc.vector.tensor_tensor(scan[:, :], scan[:, :], tmp[:, 0, :], ALU.subtract))
            own(nc.vector.tensor_tensor(scan[:, :], scan[:, :], ps_sum[:, 1, 0:NT], ALU.add))
            own(nc.vector.tensor_scalar(hist[:, :], k.has_edge[:, :], -NOWHERE, NOWHERE - 1.0, ALU.mult, ALU.add))
            own(nc.vector.tensor_tensor(scan[:, :], scan[:, :], hist[:, :], ALU.add))
            own(nc.vector.tensor_copy(k.sum_row[:, :], scan[:, :]))
            for ch in range(-(-NT // P)):
                w = min(NT - ch * P, P)
                dve.wait_ge(s_turn, -(-NT // P))
                nc.vector.tensor_copy(turned[0:w, ch, :], ps_turn[0:w, ch, :]).then_inc(s_copied, 1)

        @block.scalar
        def _(act):
            act.wait_ge(s_hist, 1)
            nc.scalar.activation(tmp[:, 1, :], tmp[:, 0, :], ACT.Sqrt).then_inc(s_root, 1)

        @block.tensor
        def _(pe):
            def step(t, b):
                pe.wait_ge(s_hot, t + 1)
                nc.tensor.matmul(ps_hist[:, 0:NT], hot_low[:, b, :], hot_high[:, b, :],
                                 start=isinstance(t, int) and t == 0,
                                 stop=isinstance(t, int) and t == ET - 1).then_inc(s_counted, 1)

            each_tile(pe, step)
            pe.wait_ge(s_hist, 1)
            nc.tensor.matmul(ps_sum[:, 0, 0:NT], k.ones[:, :], hist[:, :], start=True, stop=True)
            nc.tensor.matmul(ps_sum[:, 1, 0:NT], k.upto[:, :], hist[:, :], start=True, stop=True).then_inc(s_sums, 1)
            pe.wait_ge(s_dinv, 1)
            for ch in range(-(-NT // P)):
                w = min(NT - ch * P, P)
                nc.tensor.transpose(ps_turn[0:w, ch, :], k.dinv[:, ch * P:ch * P + w],
                                    k.ident[:, :]).then_inc(s_turn, 1)

        @block.sync
        def _(sp):
            n = -(-NT // P)
            for ch in range(n):
                w = min(NT - ch * P, P)
                sp.wait_ge(s_copied, ch + 1)
                sp.dma_start(k.dinv_dram[ch * P * P:ch * P * P + w * P, :].rearrange("(r i) o -> r (i o)", i=P),
                             turned[0:w, ch, :]).then_inc(s_out, 16)
            sp.wait_ge(s_out, 16 * n)


def sum_edges(nc, k, layer, dst):
    plan, D = k.edges, k.D
    first = layer == 0
    W = D if first else 2 * D
    with Ctx(nc, f"se{layer}") as c:
        index = c.sb("index", [P, 2, J], I32)
        X = c.sb("X", [P, 2, J, D]) if first else None
        H = c.sb("H", [P, 2, J, D])
        dv = c.sb("dv", [P, 2, J])
        dst_row = c.sb("dst_row", [P, 2, J * P], I32)
        S = c.sb("S", [P, 2, J, P])
        Q = c.sb("Q", [P, 2, J, P])
        T = c.sb("T", [P, 2, J, W])
        lastc = c.sb("lastc", [P, 2, J])
        bn = c.sb("bn", [P, J, 6])
        mv = c.sb("mv", [P, 2, J, 2])
        small = c.sb("small", [P, 2, 4, J])
        psT = [c.ps(f"psT{j}", [P, 512]) for j in range(J)]
        s_idx, s_gx, s_gd = c.sem("index_sem"), c.sems("rows_in"), c.sems("dinv_in")
        s_dr, s_S = c.sems("dst_in"), c.sem("select")
        s_var, s_root, s_scale, s_H = c.sem("var"), c.sem("root"), c.sem("scale"), c.sem("normed")
        s_mm, s_T, s_sq, s_st, s_stat = c.sem("summed"), c.sem("kept"), c.sem("squared"), c.sems("stored"), c.sem("stat")
        s_own, s_gate = c.sem("own"), c.sem("gate")
        block = c.block()
        lo, hi = 3, plan.full_groups
        OWN = 5 if first else 0

        def run(eng, step):
            sweep(eng, plan, 0, lo, hi, plan.groups, step)

        @block.gpsimd
        def _(pool):
            table = k.x_dram if first else k.msg_dram
            limit = pool.to_reg(table.shape[0] - 1)
            nodes = pool.to_reg(k.dinv_dram.shape[0] - 1)

            def step(g):
                if first:
                    wait(pool, s_H, g.number - 1)
                else:
                    wait(pool, s_T, (g.number - 1) * J)
                pool.sem_inc(s_gate, 1)
                pool.tensor_copy(index[0:g.n, g.par, 0:g.tiles],
                                 g.cols(k.src_i if first else k.slot_i)).then_inc(s_idx, 1)
                pool.wait_ge(s_idx, g.number + 1)
                pool.sem_inc(s_gate, 1)
                for j in range(g.tiles):
                    at = index[0:g.n, g.par, j:j + 1]
                    gather(pool, (X if first else H)[0:g.n, g.par, j, :], table, at, limit)\
                        .then_inc(s_gx[g.par], 16)
                    if first:
                        gather(pool, dv[0:g.n, g.par, j:j + 1], k.dinv_dram, at, nodes)\
                            .then_inc(s_gd[g.par], 16)

            run(pool, step)

        @block.sync
        def _(sp):
            def load_dst(g):
                wait(sp, s_S, g.number - 1)
                n = g.tiles * g.n
                if isinstance(g.number, int):
                    part = dst[g.number * J * P:g.number * J * P + n]
                else:
                    part = dst[bass.ds(g.number * (J * P), n)]
                sp.dma_start(dst_row[:, g.par, 0:n], part.partition_broadcast(P)).then_inc(s_dr[g.par], 16)

            def step(g):
                if g.at(1).exists:
                    load_dst(g.at(1))
                sp.wait_ge(s_T, g.tile(g.tiles - 1))
                sp.dma_start(g.rows(k.sums_dram), T[0:g.n, g.par, 0:g.tiles, 0:D]).then_inc(s_st[g.par], 16)

            load_dst(Group(plan, 0, 0))
            sweep(sp, plan, 0, lo, hi - 1, plan.groups, step)
            for b in range(2):
                sp.wait_ge(s_st[b], 16 * ((plan.groups + 1 - b) // 2))

        @block.vector
        def _(dve):
            def step(g):
                n, q, o = g.n, g.par, g.number * OWN
                wait(dve, s_T, (g.number - 1) * J)
                if not first:
                    wait(dve, s_stat, g.number - 1)
                dve.wait_ge(s_dr[q], 16 * g.half + 16)
                for j in range(g.tiles):
                    row = dst_row[:, q, j * P:j * P + n]
                    nc.vector.tensor_scalar(S[0:n, q, j, 0:n], row[0:n, :], g.col(k.dst_f, j), None, ALU.is_equal)
                    before = (k.dst_before[96:P, g.number * J + j:g.number * J + j + 1]
                              if isinstance(g.number, int) else k.dst_before[96:P, bass.ds(g.number * J + j, 1)])
                    last = nc.vector.tensor_scalar(Q[96:P, q, j, 0:n], row[96:P, :], before, None, ALU.is_equal)
                if not first:
                    last = nc.vector.tensor_scalar(lastc[0:n, q, 0:g.tiles], g.cols(k.last_f), 0.0, None, ALU.add)
                last.then_inc(s_S, 1)
                if not first:
                    return
                dve.wait_ge(s_gx[q], g.loads())
                for j in range(g.tiles):
                    last = nc.vector.bn_stats(bn[0:n, j, :], X[0:n, q, j, :])
                last.then_inc(s_own, 1)
                dve.wait_ge(s_own, o + 1)
                dve.sem_inc(s_gate, 1)
                for j in range(g.tiles):
                    last = nc.vector.bn_aggr(mv[0:n, q, j, :], bn[0:n, j, :])
                last.then_inc(s_own, 1)
                dve.wait_ge(s_own, o + 2)
                nc.vector.tensor_scalar(small[0:n, q, 0, 0:g.tiles], mv[0:n, q, 0:g.tiles, 1], EPS, None,
                                        ALU.add).then_inc(s_var, 1)
                dve.wait_ge(s_root, g.number + 1)
                nc.vector.reciprocal(small[0:n, q, 2, 0:g.tiles], small[0:n, q, 1, 0:g.tiles]).then_inc(s_own, 1)
                dve.wait_ge(s_own, o + 3)
                dve.wait_ge(s_gd[q], g.loads())
                nc.vector.tensor_tensor(small[0:n, q, 2, 0:g.tiles], small[0:n, q, 2, 0:g.tiles],
                                        dv[0:n, q, 0:g.tiles], ALU.mult).then_inc(s_own, 1)
                dve.wait_ge(s_own, o + 4)
                nc.vector.tensor_tensor(small[0:n, q, 3, 0:g.tiles], mv[0:n, q, 0:g.tiles, 0],
                                        small[0:n, q, 2, 0:g.tiles], ALU.mult).then_inc(s_own, 1)
                dve.wait_ge(s_own, o + 5)
                nc.vector.tensor_scalar(small[0:n, q, 3, 0:g.tiles], small[0:n, q, 3, 0:g.tiles], -1.0, None,
                                        ALU.mult).then_inc(s_scale, 1)

            run(dve, step)

        @block.scalar
        def _(act):
            def step(g):
                n, q = g.n, g.par
                if first:
                    act.wait_ge(s_var, g.number + 1)
                    nc.scalar.activation(small[0:n, q, 1, 0:g.tiles], small[0:n, q, 0, 0:g.tiles],
                                         ACT.Sqrt).then_inc(s_root, 1)
                    act.wait_ge(s_scale, g.number + 1)
                    wait(act, s_mm, (g.number - 1) * J)
                    for j in range(g.tiles):
                        last = nc.scalar.activation(H[0:n, q, j, :], X[0:n, q, j, :], ACT.Relu,
                                                    bias=small[0:n, q, 3, j:j + 1], scale=small[0:n, q, 2, j:j + 1])
                    last.then_inc(s_H, 1)
                wait(act, s_st[q], 16 * g.half)
                if not first:
                    wait(act, s_stat, g.number - 1)
                for j in range(g.tiles):
                    act.wait_ge(s_mm, g.tile(j))
                    nc.scalar.activation(T[0:n, q, j, 0:D], psT[j][0:n, 0:D], ACT.Copy).then_inc(s_T, 1)
                    if not first:
                        nc.scalar.activation(T[0:n, q, j, D:2 * D], psT[j][0:n, 0:D], ACT.Square).then_inc(s_sq, 1)

            run(act, step)

        @block.tensor
        def _(pe):
            freed = s_T if first else s_sq

            def step(g):
                n, q = g.n, g.par
                if first:
                    pe.wait_ge(s_H, g.number + 1)
                else:
                    pe.wait_ge(s_gx[q], g.loads())
                pe.wait_ge(s_S, g.number + 1)
                for j in range(g.tiles):
                    wait(pe, freed, (g.number - 1) * J + j + 1)
                    begin = isinstance(g.number, int) and g.number == 0 and j == 0
                    last = nc.tensor.matmul(psT[j][0:n, 0:D], S[0:n, q, j, 0:n], H[0:n, q, j, :],
                                            start=True, stop=begin)
                    if not begin:
                        pe.wait_ge(s_T, g.tile(j) - 1)
                        pq, pj = (q, j - 1) if j else (1 - q, J - 1)
                        last = nc.tensor.matmul(psT[j][0:n, 0:D], Q[96:P, q, j, 0:n], T[96:P, pq, pj, 0:D],
                                                start=False, stop=True)
                    last.then_inc(s_mm, 1)
                if first:
                    return
                for j in range(g.tiles):
                    pe.wait_ge(s_sq, g.tile(j))
                    stop = isinstance(g.number, int) and g.number == plan.groups - 1 and j == g.tiles - 1
                    begin = isinstance(g.number, int) and g.number == 0 and j == 0
                    last = nc.tensor.matmul(k.ps_stat[0:1, 0:2 * D], lastc[0:n, q, j:j + 1], T[0:n, q, j, :],
                                            start=begin, stop=stop)
                last.then_inc(s_stat, 1)

            run(pe, step)


def convolve_nodes(nc, k):
    plan, D = k.nodes, k.D
    KC = D // P
    with Ctx(nc, "cn") as c:
        index = c.sb("index", [P, 2, J], I32)
        X = c.sb("X", [P, 2, J, D])
        A = c.sb("A", [P, 2, J, D])
        Y = c.sb("Y", [P, 2, J, D])
        YT = c.sb("YT", [P, 2, J, D])
        O = c.sb("O", [P, 2, J, 2 * D])
        bn = c.sb("bn", [P, J, 6])
        mv = c.sb("mv", [P, 2, J, 2])
        small = c.sb("small", [P, 2, 4, J])
        psY = [c.ps(f"psY{j}", [P, 512]) for j in range(2)]
        psO = [c.ps(f"psO{j}", [P, 512]) for j in range(J)]
        s_x, s_a, s_idx, s_init = c.sems("x_in"), c.sems("sums_in"), c.sem("index_sem"), c.sem("init")
        s_var, s_root, s_scale, s_relu = c.sem("var"), c.sem("root"), c.sem("scale"), c.sem("relu")
        s_y, s_turn, s_yt, s_mm = c.sem("y"), c.sem("turned"), c.sem("yt"), c.sem("product")
        s_o, s_sq, s_stat, s_st = c.sem("o"), c.sem("squared"), c.sem("stat"), c.sems("stored")
        s_own, s_gate = c.sem("own"), c.sem("gate")
        block = c.block()
        lo, hi, end = 3, plan.full_groups - 2, plan.groups + 1

        def run(eng, start, step):
            sweep(eng, plan, start, lo, hi, end, step)

        @block.sync
        def _(sp):
            def step(s):
                g = s.at(2)
                if g.exists:
                    wait(sp, s_relu, g.number - 1)
                    sp.dma_start(X[0:g.n, g.par, 0:g.tiles, :], g.rows(k.x_dram)).then_inc(s_x[g.par], 16)
                g = s.at(-1)
                if g.exists:
                    sp.wait_ge(s_o, g.tile(g.tiles - 1))
                    sp.dma_start(g.rows(k.o_dram), O[0:g.n, g.par, 0:g.tiles, 0:D]).then_inc(s_st[g.par], 16)

            run(sp, -2, step)
            for b in range(2):
                sp.wait_ge(s_st[b], 16 * ((plan.groups + 1 - b) // 2))

        @block.gpsimd
        def _(pool):
            limit = pool.to_reg(k.E - 1)
            pool.memset(A[:, :, :, :], 0.0).then_inc(s_init, 1)
            pool.wait_ge(s_init, 1)

            def step(s):
                g = s.at(2)
                if not g.exists:
                    return
                wait(pool, s_y, g.number - 1)
                pool.sem_inc(s_gate, 1)
                pool.tensor_copy(index[0:g.n, g.par, 0:g.tiles], g.cols(k.sum_row)).then_inc(s_idx, 1)
                pool.wait_ge(s_idx, g.number + 1)
                pool.sem_inc(s_gate, 1)
                for j in range(g.tiles):
                    gather(pool, A[0:g.n, g.par, j, :], k.sums_dram, index[0:g.n, g.par, j:j + 1], limit)\
                        .then_inc(s_a[g.par], 16)

            run(pool, -2, step)

        @block.vector
        def _(dve):
            def step(s):
                g = s.at(-1)
                if g.exists:
                    n, q = g.n, g.par
                    wait(dve, s_stat, g.number - 1)
                    wait(dve, s_st[q], 16 * g.half)
                    for j in range(g.tiles):
                        dve.wait_ge(s_mm, g.tile(j))
                        nc.vector.scalar_tensor_tensor(O[0:n, q, j, 0:D], psO[j][0:n, 0:D], g.col(k.dinv, j),
                                                       k.bias_all[0:n, :], ALU.mult, ALU.add).then_inc(s_o, 1)
                g = s.at(1)
                if g.exists:
                    n, q = g.n, g.par
                    dve.wait_ge(s_relu, g.number + 1)
                    dve.wait_ge(s_a[q], g.loads())
                    for j in range(g.tiles):
                        last = nc.vector.scalar_tensor_tensor(Y[0:n, q, j, :], A[0:n, q, j, :], g.col(k.has_edge, j),
                                                              Y[0:n, q, j, :], ALU.mult, ALU.add)
                    last.then_inc(s_y, 1)
                g = s.at(2)
                if g.exists:
                    n, q, w, o = g.n, g.par, g.tiles, g.number * 5
                    dve.wait_ge(s_x[q], 16 * g.half + 16)
                    for j in range(w):
                        last = nc.vector.bn_stats(bn[0:n, j, :], X[0:n, q, j, :])
                    last.then_inc(s_own, 1)
                    dve.wait_ge(s_own, o + 1)
                    dve.sem_inc(s_gate, 1)
                    for j in range(w):
                        last = nc.vector.bn_aggr(mv[0:n, q, j, :], bn[0:n, j, :])
                    last.then_inc(s_own, 1)
                    dve.wait_ge(s_own, o + 2)
                    nc.vector.tensor_scalar(small[0:n, q, 0, 0:w], mv[0:n, q, 0:w, 1], EPS, None,
                                            ALU.add).then_inc(s_var, 1)
                    dve.wait_ge(s_root, g.number + 1)
                    nc.vector.reciprocal(small[0:n, q, 2, 0:w], small[0:n, q, 1, 0:w]).then_inc(s_own, 1)
                    dve.wait_ge(s_own, o + 3)
                    nc.vector.tensor_tensor(small[0:n, q, 2, 0:w], small[0:n, q, 2, 0:w], g.cols(k.dinv),
                                            ALU.mult).then_inc(s_own, 1)
                    dve.wait_ge(s_own, o + 4)
                    nc.vector.tensor_tensor(small[0:n, q, 3, 0:w], mv[0:n, q, 0:w, 0], small[0:n, q, 2, 0:w],
                                            ALU.mult).then_inc(s_own, 1)
                    dve.wait_ge(s_own, o + 5)
                    nc.vector.tensor_scalar(small[0:n, q, 3, 0:w], small[0:n, q, 3, 0:w], -1.0, None,
                                            ALU.mult).then_inc(s_scale, 1)

            run(dve, -2, step)

        @block.scalar
        def _(act):
            def step(s):
                now, ahead, behind = s, s.at(1), s.at(-1)
                for j in range(J):
                    if now.exists and j < now.tiles:
                        act.wait_ge(s_turn, now.tile(j))
                        wait(act, s_mm, (now.number - 2) * J + j + 1)
                        nc.scalar.activation(YT[:, now.par, j, :].rearrange("p (c n) -> p c n", c=KC)[:, :, 0:now.n],
                                             psY[j % 2][:, 0:D].rearrange("p (c n) -> p c n", c=KC)[:, :, 0:now.n],
                                             ACT.Copy).then_inc(s_yt, 1)
                    if ahead.exists and j < ahead.tiles:
                        n, q = ahead.n, ahead.par
                        if j == 0:
                            act.wait_ge(s_scale, ahead.number + 1)
                            wait(act, s_turn, (ahead.number - 1) * J)
                        last = nc.scalar.activation(Y[0:n, q, j, :], X[0:n, q, j, :], ACT.Relu,
                                                    bias=small[0:n, q, 3, j:j + 1], scale=small[0:n, q, 2, j:j + 1])
                        if j == ahead.tiles - 1:
                            last.then_inc(s_relu, 1)
                    if behind.exists and j < behind.tiles:
                        n, q = behind.n, behind.par
                        act.wait_ge(s_o, behind.tile(j))
                        nc.scalar.activation(O[0:n, q, j, D:2 * D], O[0:n, q, j, 0:D], ACT.Square).then_inc(s_sq, 1)
                g = s.at(2)
                if g.exists:
                    act.wait_ge(s_var, g.number + 1)
                    nc.scalar.activation(small[0:g.n, g.par, 1, 0:g.tiles], small[0:g.n, g.par, 0, 0:g.tiles],
                                         ACT.Sqrt).then_inc(s_root, 1)

            run(act, -2, step)

        @block.tensor
        def _(pe):
            def turn(g, j):
                n, q = g.n, g.par
                if j == 0:
                    pe.wait_ge(s_y, g.number + 1)
                wait(pe, s_yt, g.tile(j) - 2 if j >= 2 else g.number * J - j)
                for kc in range(KC):
                    last = nc.tensor.transpose(psY[j % 2][:, kc * P:kc * P + n], Y[0:n, q, j, kc * P:(kc + 1) * P],
                                               k.ident[0:n, 0:n])
                last.then_inc(s_turn, 1)

            def product(g, j):
                n, q = g.n, g.par
                pe.wait_ge(s_yt, g.tile(j))
                wait(pe, s_o, (g.number - 1) * J + j + 1)
                for kc in range(KC):
                    last = nc.tensor.matmul(psO[j][0:n, 0:D], YT[:, q, j, kc * P:kc * P + n], k.w0[:, kc, :],
                                            start=kc == 0, stop=kc == KC - 1)
                last.then_inc(s_mm, 1)

            def step(s):
                g = s
                if g.exists:
                    turn(g, 0)
                    for j in range(g.tiles):
                        if j + 1 < g.tiles:
                            turn(g, j + 1)
                        product(g, j)
                g = s.at(-1)
                if g.exists:
                    for j in range(g.tiles):
                        pe.wait_ge(s_sq, g.tile(j))
                        begin = isinstance(g.number, int) and g.number == 0 and j == 0
                        stop = isinstance(g.number, int) and g.number == plan.groups - 1 and j == g.tiles - 1
                        last = nc.tensor.matmul(k.ps_stat[0:1, 0:2 * D], k.ones[0:g.n, 0:1], O[0:g.n, g.par, j, :],
                                                start=begin, stop=stop)
                    last.then_inc(s_stat, 1)

            run(pe, -2, step)


def column_norm(nc, k, layer, gamma, beta, coef):
    D, N = k.D, k.N
    with Ctx(nc, f"bc{layer}") as c:
        gb = c.sb("gb", [1, 2, D])
        stat = c.sb("stat", [1, 2 * D])
        row = c.sb("row", [1, 2 * D])
        t = c.sb("t", [1, 3, D])
        ps = c.ps("ps", [P, 512])
        s_in, s_own, s_var, s_root, s_row, s_all = [c.sem(n) for n in ("in", "own", "var", "root", "row_sem", "all")]
        s_done = c.sem("done")
        block = c.block()

        @block.sync
        def _(sp):
            sp.dma_start(gb[0:1, 0, :], gamma.rearrange("(a d) -> a d", a=1)).then_inc(s_in, 16)
            sp.dma_start(gb[0:1, 1, :], beta.rearrange("(a d) -> a d", a=1)).then_inc(s_in, 16)

        @block.vector
        def _(dve):
            own = Chain(dve, s_own)
            own(nc.vector.tensor_scalar(stat[:, :], k.ps_stat[0:1, 0:2 * D], 1.0 / N, None, ALU.mult))
            own(nc.vector.tensor_tensor(t[:, 0, :], stat[:, 0:D], stat[:, 0:D], ALU.mult))
            own(nc.vector.tensor_tensor(t[:, 0, :], stat[:, D:2 * D], t[:, 0, :], ALU.subtract))
            nc.vector.tensor_scalar(t[:, 0, :], t[:, 0, :], 0.0, EPS, ALU.max, ALU.add).then_inc(s_var, 1)
            dve.wait_ge(s_root, 1)
            own(nc.vector.reciprocal(t[:, 2, :], t[:, 1, :]))
            dve.wait_ge(s_in, 32)
            own(nc.vector.tensor_tensor(row[:, 0:D], t[:, 2, :], gb[0:1, 0, :], ALU.mult))
            own(nc.vector.tensor_tensor(t[:, 0, :], row[:, 0:D], stat[:, 0:D], ALU.mult))
            nc.vector.tensor_tensor(row[:, D:2 * D], gb[0:1, 1, :], t[:, 0, :], ALU.subtract).then_inc(s_row, 1)
            dve.wait_ge(s_all, 1)
            nc.vector.tensor_copy(coef[:, :], ps[:, 0:2 * D]).then_inc(s_done, 1)

        @block.scalar
        def _(act):
            act.wait_ge(s_var, 1)
            nc.scalar.activation(t[:, 1, :], t[:, 0, :], ACT.Sqrt).then_inc(s_root, 1)

        @block.tensor
        def _(pe):
            pe.wait_ge(s_row, 1)
            nc.tensor.matmul(ps[:, 0:2 * D], k.ones[0:1, :], row[0:1, :], start=True, stop=True).then_inc(s_all, 1)


def relate_messages(nc, k):
    plan, D = k.slots, k.D
    KC = D // P
    OWN = 18
    with Ctx(nc, "rm") as c:
        index = c.sb("index", [P, 2, J], I32)
        X = c.sb("X", [P, 2, J, D])
        O = c.sb("O", [P, 2, J, D])
        H = c.sb("H", [P, 2, J, D])
        HT = c.sb("HT", [P, 2, J, D])
        M = c.sb("M", [P, 2, J, D])
        bn = c.sb("bn", [P, J, 6])
        mv = c.sb("mv", [P, 2, J, 2])
        root = c.sb("root", [P, 4, J])
        half = c.sb("half", [P, 2, J], I32)
        small = c.sb("small", [P, 2, 2, J])
        psH = [c.ps(f"psH{j}", [P, 512]) for j in range(2)]
        psM = [c.ps(f"psM{j}", [P, 512]) for j in range(2)]
        s_x, s_ob, s_idx, s_gate, s_own = c.sems("x_in"), c.sems("o_in"), c.sem("index_sem"), c.sem("gate"), c.sem("own")
        s_scaled = c.sem("scaled")
        s_z, s_th, s_scale, s_relu = c.sem("z"), c.sem("tanh"), c.sem("scale"), c.sem("relu")
        s_turn, s_ht, s_mm, s_m, s_st = c.sem("turned"), c.sem("ht"), c.sem("product"), c.sem("m"), c.sems("stored")
        block = c.block()
        lo, hi, end = 3, plan.full_groups - 1, plan.groups

        def run(eng, start, step):
            sweep(eng, plan, start, lo, hi, end, step)

        @block.gpsimd
        def _(pool):
            limit = pool.to_reg(k.N - 1)

            def step(g):
                if not g.exists:
                    return
                wait(pool, s_relu, g.number - 1)
                pool.sem_inc(s_gate, 1)
                pool.tensor_copy(index[:, g.par, :], g.cols(k.slot_src)).then_inc(s_idx, 1)
                pool.wait_ge(s_idx, g.number + 1)
                pool.sem_inc(s_gate, 1)
                for j in range(g.tiles):
                    gather(pool, O[:, g.par, j, :], k.o_dram, index[:, g.par, j:j + 1], limit)\
                        .then_inc(s_ob[g.par], 16)
                for j in range(g.tiles):
                    gather(pool, X[:, g.par, j, :], k.x_dram, index[:, g.par, j:j + 1], limit)\
                        .then_inc(s_x[g.par], 16)

            run(pool, 0, step)

        @block.sync
        def _(sp):
            def step(g):
                sp.wait_ge(s_m, g.tile(g.tiles - 1))
                sp.dma_start(g.rows(k.msg_dram), M[:, g.par, :, :]).then_inc(s_st[g.par], 16)

            run(sp, 0, step)
            for b in range(2):
                sp.wait_ge(s_st[b], 16 * ((plan.groups + 1 - b) // 2))

        @block.vector
        def _(dve):
            def step(s):
                g = s.at(1)
                if g.exists:
                    q = g.par
                    dve.wait_ge(s_ob[q], g.loads())
                    nc.vector.tensor_tensor(O[:, q, :, :], O[:, q, :, :],
                                            k.coef0[:, 0:D].unsqueeze(1).broadcast_to([P, J, D]), ALU.mult)\
                        .then_inc(s_scaled, 1)
                    dve.wait_ge(s_scaled, g.number + 1)
                    nc.vector.tensor_tensor(O[:, q, :, :], O[:, q, :, :],
                                            k.coef0[:, D:2 * D].unsqueeze(1).broadcast_to([P, J, D]), ALU.add)\
                        .then_inc(s_z, 1)
                g = s
                if not g.exists:
                    return
                q = g.par
                dve.wait_ge(s_th, g.number + 1)
                dve.wait_ge(s_x[q], g.loads())
                v, t = root[:, 0, :], root[:, 2, :]
                V = nc.vector

                def own(ins, n):
                    ins.then_inc(s_own, 1)
                    dve.wait_ge(s_own, g.number * OWN + n)

                own(V.tensor_tensor(X[:, q, :, :], X[:, q, :, :], O[:, q, :, :], ALU.add), 1)
                for j in range(J):
                    last = V.bn_stats(bn[:, j, :], X[:, q, j, :])
                own(last, 2)
                dve.sem_inc(s_gate, 1)
                for j in range(J):
                    last = V.bn_aggr(mv[:, q, j, :], bn[:, j, :])
                own(last, 3)
                own(V.tensor_scalar(v, mv[:, q, :, 1], EPS, None, ALU.add), 4)
                own(V.tensor_scalar(half[:, 0, :], v.bitcast(I32), 1, None, ALU.arith_shift_right), 5)
                own(V.tensor_scalar(half[:, 1, :], half[:, 0, :], -1.0, float(0x5F3759DF), ALU.mult, ALU.add), 6)
                y = half[:, 1, :].bitcast(F32)
                n = 6
                for it in range(4):
                    own(V.scalar_tensor_tensor(t, y, -0.5, y, ALU.mult, ALU.mult), n + 1)
                    own(V.tensor_tensor(t, t, v, ALU.mult), n + 2)
                    n += 2
                    out = small[:, q, 0, :] if it == 3 else root[:, 1 + 2 * (it % 2), :]
                    own(V.scalar_tensor_tensor(out, t, 1.5, y, ALU.add, ALU.mult), n + 1)
                    n += 1
                    y = out
                V.scalar_tensor_tensor(small[:, q, 1, :], mv[:, q, :, 0], -1.0, small[:, q, 0, :],
                                       ALU.mult, ALU.mult).then_inc(s_scale, 1)

            run(dve, -1, step)

        @block.scalar
        def _(act):
            def step(s):
                g = s.at(1)
                if g.exists:
                    act.wait_ge(s_z, g.number + 1)
                    nc.scalar.activation(O[:, g.par, :, :], O[:, g.par, :, :], ACT.Tanh).then_inc(s_th, 1)
                g = s
                if not g.exists:
                    return
                q = g.par
                act.wait_ge(s_scale, g.number + 1)
                wait(act, s_turn, (g.number - 1) * J)
                for j in range(J):
                    last = nc.scalar.activation(H[:, q, j, :], X[:, q, j, :], ACT.Relu,
                                                bias=small[:, q, 1, j:j + 1], scale=small[:, q, 0, j:j + 1])
                last.then_inc(s_relu, 1)
                wait(act, s_st[q], 16 * g.half)
                for j in range(J + 1):
                    if j < J:
                        act.wait_ge(s_turn, g.tile(j))
                        wait(act, s_mm, (g.number - 2) * J + j + 1)
                        nc.scalar.activation(HT[:, q, j, :], psH[j % 2][:, 0:D], ACT.Copy).then_inc(s_ht, 1)
                    if j:
                        act.wait_ge(s_mm, g.tile(j - 1))
                        nc.scalar.activation(M[:, q, j - 1, :], psM[(j - 1) % 2][:, 0:D], ACT.Copy).then_inc(s_m, 1)

            run(act, -1, step)

        @block.tensor
        def _(pe):
            def turn(g, j):
                if j == 0:
                    pe.wait_ge(s_relu, g.number + 1)
                wait(pe, s_ht, g.tile(j) - 2 if j >= 2 else g.number * J - j)
                for kc in range(KC):
                    last = nc.tensor.transpose(psH[j % 2][:, kc * P:(kc + 1) * P],
                                               H[:, g.par, j, kc * P:(kc + 1) * P], k.ident[:, :])
                last.then_inc(s_turn, 1)

            def product(g, j):
                col = g.number * J + j
                off = pe.value_load(k.tile_weight[0:1, col:col + 1] if isinstance(col, int)
                                    else k.tile_weight[0:1, bass.ds(col, 1)], min_val=0, max_val=(RELS - 1) * D)
                pe.wait_ge(s_ht, g.tile(j))
                wait(pe, s_m, g.tile(j) - 2 if j >= 2 else g.number * J - j)
                for kc in range(KC):
                    last = nc.tensor.matmul(psM[j % 2][:, 0:D], HT[:, g.par, j, kc * P:(kc + 1) * P],
                                            k.w1[:, kc, bass.ds(off, D)], start=kc == 0, stop=kc == KC - 1)
                last.then_inc(s_mm, 1)

            def step(g):
                turn(g, 0)
                for j in range(J):
                    if j + 1 < J:
                        turn(g, j + 1)
                    product(g, j)

            run(pe, 0, step)


def finish_nodes(nc, k, out):
    plan, D = k.nodes, k.D
    with Ctx(nc, "fn") as c:
        index = c.sb("index", [P, 2, J], I32)
        X = c.sb("X", [P, 2, J, D])
        Z = c.sb("Z", [P, 2, J, D])
        A = c.sb("A", [P, 2, J, D])
        R = c.sb("R", [P, 2, J, D])
        psR = [c.ps(f"psR{j}", [P, 512]) for j in range(J)]
        s_x, s_ob, s_a, s_st = c.sems("x_in"), c.sems("o_in"), c.sems("sums_in"), c.sems("stored")
        s_idx, s_init, s_gate, s_own = c.sem("index_sem"), c.sem("init"), c.sem("gate"), c.sem("own")
        s_z, s_th, s_u, s_mm, s_r = c.sem("z"), c.sem("tanh"), c.sem("scaled"), c.sem("summed"), c.sem("result")
        block = c.block()
        lo, hi, end = 3, plan.full_groups - 2, plan.groups + 1

        def run(eng, start, step):
            sweep(eng, plan, start, lo, hi, end, step)

        @block.sync
        def _(sp):
            def step(s):
                g = s.at(2)
                if g.exists:
                    wait(sp, s_mm, (g.number - 1) * J)
                    sp.dma_start(Z[0:g.n, g.par, 0:g.tiles, :], g.rows(k.o_dram)).then_inc(s_ob[g.par], 16)
                g = s.at(1)
                if g.exists:
                    wait(sp, s_r, (g.number - 1) * J)
                    sp.dma_start(X[0:g.n, g.par, 0:g.tiles, :], g.rows(k.x_dram)).then_inc(s_x[g.par], 16)
                g = s.at(-1)
                if g.exists:
                    sp.wait_ge(s_r, g.tile(g.tiles - 1))
                    sp.dma_start(g.rows(out), R[0:g.n, g.par, 0:g.tiles, :]).then_inc(s_st[g.par], 16)

            run(sp, -2, step)
            for b in range(2):
                sp.wait_ge(s_st[b], 16 * ((plan.groups + 1 - b) // 2))

        @block.gpsimd
        def _(pool):
            limit = pool.to_reg(k.E - 1)
            pool.memset(A[:, :, :, :], 0.0).then_inc(s_init, 1)
            pool.wait_ge(s_init, 1)

            def step(s):
                g = s.at(1)
                if not g.exists:
                    return
                wait(pool, s_mm, (g.number - 1) * J)
                pool.sem_inc(s_gate, 1)
                pool.tensor_copy(index[0:g.n, g.par, 0:g.tiles], g.cols(k.sum_row)).then_inc(s_idx, 1)
                pool.wait_ge(s_idx, g.number + 1)
                pool.sem_inc(s_gate, 1)
                for j in range(g.tiles):
                    gather(pool, A[0:g.n, g.par, j, :], k.sums_dram, index[0:g.n, g.par, j:j + 1], limit)\
                        .then_inc(s_a[g.par], 16)

            run(pool, -2, step)

        @block.vector
        def _(dve):
            def step(s):
                g = s.at(1)
                if g.exists:
                    n, q, w = g.n, g.par, g.tiles
                    dve.wait_ge(s_ob[q], 16 * g.half + 16)
                    nc.vector.tensor_tensor(Z[0:n, q, 0:w, :], Z[0:n, q, 0:w, :],
                                            k.coef0[0:n, 0:D].unsqueeze(1).broadcast_to([n, w, D]), ALU.mult)\
                        .then_inc(s_own, 1)
                    dve.wait_ge(s_own, g.number + 1)
                    nc.vector.tensor_tensor(Z[0:n, q, 0:w, :], Z[0:n, q, 0:w, :],
                                            k.coef0[0:n, D:2 * D].unsqueeze(1).broadcast_to([n, w, D]), ALU.add)\
                        .then_inc(s_z, 1)
                g = s
                if g.exists:
                    n, q = g.n, g.par
                    dve.wait_ge(s_a[q], g.loads())
                    for j in range(g.tiles):
                        last = nc.vector.scalar_tensor_tensor(A[0:n, q, j, :], A[0:n, q, j, :], g.col(k.has_edge, j),
                                                              k.coef1[0:n, 0:D], ALU.mult, ALU.mult)
                    last.then_inc(s_u, 1)
                g = s.at(-1)
                if g.exists:
                    n, q = g.n, g.par
                    dve.wait_ge(s_x[q], 16 * g.half + 16)
                    wait(dve, s_st[q], 16 * g.half)
                    for j in range(g.tiles):
                        dve.wait_ge(s_mm, g.tile(j))
                        nc.vector.tensor_tensor(R[0:n, q, j, :], psR[j][0:n, 0:D], X[0:n, q, j, :],
                                                ALU.add).then_inc(s_r, 1)

            run(dve, -2, step)

        @block.scalar
        def _(act):
            def step(s):
                g = s.at(1)
                if g.exists:
                    act.wait_ge(s_z, g.number + 1)
                    nc.scalar.activation(Z[0:g.n, g.par, 0:g.tiles, :], Z[0:g.n, g.par, 0:g.tiles, :],
                                         ACT.Tanh).then_inc(s_th, 1)

            run(act, -2, step)

        @block.tensor
        def _(pe):
            def step(g):
                if not g.exists:
                    return
                n, q = g.n, g.par
                pe.wait_ge(s_th, g.number + 1)
                pe.wait_ge(s_u, g.number + 1)
                for j in range(g.tiles):
                    wait(pe, s_r, (g.number - 1) * J + j + 1)
                    nc.tensor.matmul(psR[j][0:n, 0:D], k.ones[0:1, 0:n], k.coef1[0:1, D:2 * D], start=True, stop=False)
                    nc.tensor.matmul(psR[j][0:n, 0:D], k.ident[0:n, 0:n], Z[0:n, q, j, :], start=False, stop=False)
                    nc.tensor.matmul(psR[j][0:n, 0:D], k.ident[0:n, 0:n], A[0:n, q, j, :], start=False,
                                     stop=True).then_inc(s_mm, 1)

            run(pe, -2, step)


class Names:
    pass


def build(nc, x, src, dst, rel, w0, b0, g0, be0, w1, g1, be1, consts, out):
    k = Names()
    k.N, k.D = x.shape
    k.E = src.shape[0]
    D = k.D
    k.nodes, k.edges = Plan(k.N), Plan(k.E)
    slot_tiles = (k.E + RELS * (P - 1)) // P
    slot_tiles = -(-slot_tiles // J) * J
    k.slots = Plan(slot_tiles * P)
    k.node_cols = k.N // P + 1
    ET, BT, NT = k.edges.tiles, k.slots.tiles, k.node_cols
    k.x_dram = x
    dram = lambda name, shape, dt: nc.dram_tensor(name, shape, dt, kind="Internal").ap()
    k.slot_src_dram = dram("slot_src_dram", (P * BT, 1), I32)
    k.dinv_dram = dram("dinv_dram", (NT * P, 1), F32)
    k.sums_dram = dram("sums_dram", (k.E, D), F32)
    k.o_dram = dram("o_dram", (k.N, D), F32)
    k.msg_dram = dram("msg_dram", (BT * P, D), F32)
    with Ctx(nc, "k") as c:
        k.ident, k.ones, k.below, k.upto = (c.sb(n, [P, P]) for n in ("ident", "ones", "below", "upto"))
        k.iota = c.sb("iota", [P, 512])
        k.is_last = c.sb("is_last", [P, 2])
        k.w0 = c.sb("w0", [P, D // P, D])
        k.w1 = c.sb("w1", [P, D // P, RELS * D])
        k.bias_all = c.sb("bias_all", [P, D])
        k.src_f, k.dst_f, k.last_f, k.dst_high, k.dst_low, k.dst_before = (
            c.sb(n, [P, ET]) for n in ("src_f", "dst_f", "last_f", "dst_high", "dst_low", "dst_before"))
        k.src_i, k.slot_i = (c.sb(n, [P, ET], I32) for n in ("src_i", "slot_i"))
        k.slot_src, k.tile_weight = (c.sb(n, [P, BT], I32) for n in ("slot_src", "tile_weight"))
        k.dinv, k.has_edge = (c.sb(n, [P, NT]) for n in ("dinv_t", "has_edge"))
        k.sum_row = c.sb("sum_row", [P, NT], I32)
        k.coef0, k.coef1 = c.sb("coef0", [P, 2 * D]), c.sb("coef1", [P, 2 * D])
        k.ps_stat = c.ps("ps_stat", [P, 512])
        k.const_loads = [
            (consts[0], k.ident[:, :]), (consts[1], k.ones[:, :]), (consts[2], k.below[:, :]),
            (consts[3], k.upto[:, :]), (consts[4], k.iota[:, :]), (consts[5], k.is_last[:, :]),
            (w0.rearrange("(c p) o -> p c o", p=P), k.w0[:, :, :]),
            (b0.partition_broadcast(P), k.bias_all[:, :])]
        k.const_loads += [(w1[r].rearrange("(c p) o -> p c o", p=P), k.w1[:, :, r * D:(r + 1) * D]) for r in range(RELS)]
        edge_tables(nc, k, src, dst, rel)
        degree_tables(nc, k)
        sum_edges(nc, k, 0, dst)
        convolve_nodes(nc, k)
        column_norm(nc, k, 0, g0, be0, k.coef0)
        relate_messages(nc, k)
        sum_edges(nc, k, 1, dst)
        column_norm(nc, k, 1, g1, be1, k.coef1)
        finish_nodes(nc, k, out)


_INS = ['x', 'src', 'dst', 'edge_type_8', 'L0_gnn_W', 'L0_gnn_b', 'L0_gnn_gamma', 'L0_gnn_beta',
        'L1_gnn_weight', 'L1_gnn_gamma', 'L1_gnn_beta']


def kernel(**inputs):
    import numpy as _np
    import concourse.bacc as _bacc
    from concourse import mybir as _mybir
    from concourse.bass_utils import run_bass_kernel_spmd as _run

    nc = _bacc.Bacc("TRN2", target_bir_lowering=False, num_devices=1)
    arrays, args = {}, []

    def given(name, a):
        arrays[name] = a
        return nc.dram_tensor(name, a.shape, _mybir.dt.from_np(a.dtype), kind="ExternalInput").ap()

    for name in _INS:
        args.append(given(f"in_{name}_dram", _np.ascontiguousarray(inputs[name])))
    n = _np.arange(P)
    last = (n == P - 1).astype(_np.float32)
    shapes_only = [
        _np.eye(P, dtype=_np.float32), _np.ones((P, P), _np.float32),
        (n[:, None] < n[None, :]).astype(_np.float32), (n[:, None] <= n[None, :]).astype(_np.float32),
        _np.tile(_np.arange(512, dtype=_np.float32), (P, 1)), _np.stack([last, last - 1], 1)]
    args.append([given(f"const_{i}_dram", _np.ascontiguousarray(a)) for i, a in enumerate(shapes_only)])
    shape = inputs['x'].shape
    args.append(nc.dram_tensor("out_0_dram", shape, _mybir.dt.float32, kind="ExternalOutput").ap())
    build(nc, *args)
    r = _run(nc, [arrays], core_ids=[0])
    return r.results[0]["out_0_dram"]
```

```python
from contextlib import ExitStack

import concourse.bass as bass
from concourse import mybir

F32 = mybir.dt.float32
BF16 = mybir.dt.bfloat16
I32 = mybir.dt.int32
ALU = mybir.AluOpType
ACT = mybir.ActivationFunctionType

P = 128
J = 3
NB = 4
RELS = 8
EPS = 1e-5
EARLY = 4
NOWHERE = 1.0e6


class Plan:

    def __init__(self, rows):
        self.rows = rows
        self.full_tiles, self.tail = divmod(rows, P)
        assert self.full_tiles % J == 0
        self.full_groups = self.full_tiles // J
        self.groups = self.full_groups + (self.tail > 0)
        self.tiles = self.full_tiles + (self.tail > 0)


class Group:

    def __init__(self, plan, loop, r):
        self.plan, self.loop, self.r = plan, loop, r
        static = isinstance(loop, int)
        self.number = NB * loop + r
        self.half = loop + r // NB
        self.par = r % NB
        self.side = r % 2
        self.exists = not static or 0 <= r < plan.groups
        short = static and r == plan.full_groups
        self.tiles = 1 if short else J
        self.n = plan.tail if short else P

    def at(self, d):
        return Group(self.plan, self.loop, self.r + d)

    def rows(self, dram):
        count = self.tiles * self.n
        if isinstance(self.number, int):
            part = dram[self.number * J * P:self.number * J * P + count, :]
        else:
            part = dram[bass.ds(self.number * (J * P), count), :]
        return part.rearrange("(j p) d -> p j d", p=self.n)

    def cols(self, table, n=None):
        n = self.n if n is None else n
        if isinstance(self.number, int):
            return table[0:n, self.number * J:self.number * J + self.tiles]
        return table[0:n, bass.ds(self.number * J, self.tiles)]

    def col(self, table, j, n=None):
        n = self.n if n is None else n
        if isinstance(self.number, int):
            return table[0:n, self.number * J + j:self.number * J + j + 1]
        return table[0:n, bass.ds(self.number * J + j, 1)]

    def tile(self, j):
        return self.number * J + (j + 1)

    def loads(self, each=1):
        return self.half * (16 * J * each) + 16 * self.tiles * each


def sweep(eng, plan, start, lo, hi, end, step):
    turns = max(0, (hi - lo) // NB)
    for r in range(start, lo if turns else end):
        step(Group(plan, 0, r))
    if turns:
        with eng.Fori(0, turns) as i:
            for u in range(NB):
                step(Group(plan, i, lo + u))
        for r in range(lo + NB * turns, end):
            step(Group(plan, 0, r))


def all_stored(sp, sems, plan):
    for b in range(NB):
        sp.wait_ge(sems[b], 16 * ((plan.groups + NB - 1 - b) // NB))


def wait(eng, sem, value):
    if isinstance(value, int) and value <= 0:
        return
    eng.wait_ge(sem, value)


class Ctx:

    def __init__(self, nc, name, whole=None):
        self.nc, self.name, self.stack, self.whole = nc, name, ExitStack(), whole
        self.used = []

    def __enter__(self):
        self.stack.__enter__()
        return self

    def __exit__(self, *a):
        return self.stack.__exit__(*a)

    def sb(self, name, shape, dt=F32):
        return self.stack.enter_context(self.nc.sbuf_tensor(f"{self.name}_{name}", shape, dt))

    def ps(self, name, shape):
        return self.stack.enter_context(self.nc.psum_tensor(f"{self.name}_{name}", shape, F32))

    def sem(self, name):
        self.used.append(self.stack.enter_context(self.nc.semaphore(f"{self.name}_{name}")))
        return self.used[-1]

    def sems(self, name):
        return [self.sem(f"{name}{k}") for k in range(NB)]

    def pool_sems(self, name, count=NB):
        return [self.whole.sem(f"{self.name}_{name}{k}") for k in range(count)]

    def clear(self):
        for s in self.used:
            self.nc.gpsimd.sem_clear(s)
        self.nc.all_engine_barrier()

    def block(self):
        self.stack.callback(self.clear)
        return self.stack.enter_context(self.nc.Block())


class Chain:

    def __init__(self, eng, sem, base=0):
        self.eng, self.sem, self.base, self.n = eng, sem, base, 0

    def __call__(self, ins):
        self.n += 1
        ins.then_inc(self.sem, 1)
        self.eng.wait_ge(self.sem, self.base + self.n)


def gather(pool, out, table, index, limit):
    return pool.indirect_dma_start(
        out=out, out_offset=None, in_=table[:, :],
        in_offset=bass.IndirectOffsetOnAxis(ap=index, axis=0), bounds_check=limit, oob_is_err=False)


class Scatter:

    def __init__(self, c, k, first):
        self.k, self.first = k, first
        self.pair = c.sb("slot_pair", [P, 2, J, 2], I32)
        self.s_put = c.pool_sems("scattered", 2)
        self.s_copied, self.s_gate = c.sem("pair_copied"), c.sem("scatter_gate")

    def put(self, pool, limit, group, b, half, tiles=J):
        at = (group + self.first) * J
        span = slice(at, at + tiles) if isinstance(at, int) else bass.ds(at, tiles)
        wait(pool, self.s_put[b], half * (16 * J))
        pool.sem_inc(self.s_gate, 1)
        pool.tensor_copy(self.pair[:, b, 0:tiles, 0], self.k.src_i[:, span]).then_inc(self.s_copied, 1)
        pool.tensor_copy(self.pair[:, b, 0:tiles, 1], self.k.slot_at[:, span]).then_inc(self.s_copied, 1)
        pool.wait_ge(self.s_copied, 2 * group + 2)
        pool.sem_inc(self.s_gate, 1)
        for j in range(tiles):
            pool.indirect_dma_start(
                out=self.k.slot_src_dram[:, :],
                out_offset=bass.IndirectOffsetOnAxis(ap=self.pair[:, b, j, 1:2], axis=0),
                in_=self.pair[:, b, j, 0:1], in_offset=None, bounds_check=limit,
                oob_is_err=False).then_inc(self.s_put[b], 16)

    def landed(self, eng, groups, tail=0):
        for b in range(2):
            tiles = J * len(range(b, groups, 2)) + (tail if groups % 2 == b else 0)
            wait(eng, self.s_put[b], 16 * tiles)


def stage_indices(nc, dve, g, index, table, s_gate, s_idx):
    if g.exists:
        dve.sem_inc(s_gate, 1)
        nc.vector.tensor_copy(index[0:g.n, g.par, 0:g.tiles], g.cols(table)).then_inc(s_idx, 1)


def order_edges(nc, k, src, dst, rel):
    E = k.E
    C = -(-E // P)
    DIGIT = 3
    BINS = 1 << DIGIT
    PASSES = -(-k.N.bit_length() // DIGIT)
    OWN = 11 + 4 * BINS
    rows_dram = nc.dram_tensor("sort_rows", (P * C, 4), I32, kind="Internal").ap()
    with Ctx(nc, "oe", k.whole) as c:
        raw = c.sb("raw", [P, 4, C], I32)
        late = c.sb("late", [P, C])
        unsorted = c.sb("unsorted", [P, 1])
        flag = c.sb("flag", [P, 1], I32)
        rows = c.sb("rows", [P, C, 4], I32)
        digit_i = c.sb("digit_i", [P, C], I32)
        digit = c.sb("digit", [P, C])
        zeros = c.sb("zeros", [P, C])
        mask = c.sb("mask", [P, BINS, C])
        run = c.sb("run", [P, BINS, C])
        total = c.sb("total", [P, BINS])
        base = c.sb("base", [P, 3, BINS])
        place = c.sb("place", [P, C])
        place_i = c.sb("place_i", [P, C], I32)
        put_at = c.sb("put_at", [P, 1], I32)
        put_row = c.sb("put_row", [P, 4], I32)
        ps = c.ps("ps", [P, 512])
        s_const, s_pad, s_raw, s_copied = c.sem("constants"), c.sem("padded"), c.sem("raw_sem"), c.sem("copied")
        s_late, s_sum, s_flag, s_gate = c.sem("late_sem"), c.sem("sum"), c.sem("flag_sem"), c.sem("gate")
        s_made, s_listed, s_whole, s_loaded = c.sem("rows_made"), c.sem("listed"), c.sem("whole"), c.sem("loaded")
        s_own, s_total, s_before, s_place = c.sem("own"), c.sem("totals"), c.sem("before"), c.sem("places")
        s_stage, s_put, s_split, s_out = c.sem("staged"), c.pool_sems("put", 1)[0], c.sem("split"), c.sem("out")
        block = c.block()
        lists = [(dst, 1, E - 1), (dst, 0, E), (src, 0, E), (rel, 0, E)]
        loads = sum((n // C > 0) + (n % C > 0) for _, _, n in lists)

        def parts(a, first, n, kind):
            full, rest = divmod(n, C)
            pairs = [(a[first:first + full * C].rearrange("(r i) -> r i", i=C), raw[0:full, kind, :])] if full else []
            if rest:
                pairs.append((a[first + full * C:first + n].rearrange("(r i) -> r i", r=1),
                              raw[full:full + 1, kind, 0:rest]))
            return pairs

        @block.sync
        def _(sp):
            for dram, there in k.const_loads:
                sp.dma_start(there, dram).then_inc(s_const, 16)
            sp.wait_ge(s_pad, 4)
            for kind, (a, first, n) in enumerate(lists):
                for there, here in parts(a, first, n, kind):
                    sp.dma_start(here, there).then_inc(s_raw, 16)
            for a, copy in ((src, k.src_list), (dst, k.dst_list), (rel, k.rel_list)):
                sp.dma_start(copy, a).then_inc(s_copied, 16)
            for dram, there in k.weight_loads:
                sp.dma_start(there, dram).then_inc(k.s_weights, 16)
            sp.wait_ge(s_copied, 48)
            sp.wait_ge(s_flag, 1)
            out_of_order = sp.value_load(flag[0:1, 0:1], min_val=0, max_val=P * C)
            with sp.If(out_of_order > 0):
                sp.wait_ge(s_made, 1)
                sp.dma_start(rows_dram.rearrange("(p t) f -> p t f", p=P), rows[:, :, :]).then_inc(s_listed, 16)
                with sp.Fori(0, PASSES + 1) as i:
                    sp.wait_ge(s_whole, i + 1)
                    sp.dma_start(rows[:, :, :], rows_dram.rearrange("(p t) f -> p t f", p=P)).then_inc(s_loaded, 16)
                sp.wait_ge(s_split, 1)
                for kind, a in ((1, k.dst_list), (2, k.src_list), (3, k.rel_list)):
                    for there, here in parts(a, 0, E, kind):
                        sp.dma_start(there, here).then_inc(s_out, 16)
                sp.wait_ge(s_out, 16 * 3 * ((E // C > 0) + (E % C > 0)))
            sp.wait_ge(s_const, 16 * len(k.const_loads))

        @block.gpsimd
        def _(pool):
            for kind, fill in enumerate((k.N, k.N, 0, RELS)):
                pool.memset(raw[:, kind, :], fill).then_inc(s_pad, 1)
            limit = pool.to_reg(P * C - 1)
            pool.wait_ge(s_flag, 1)
            out_of_order = pool.value_load(flag[0:1, 0:1], min_val=0, max_val=P * C)
            with pool.If(out_of_order > 0):
                pool.wait_ge(s_listed, 16)
                pool.sem_inc(s_whole, 1)
                with pool.Fori(0, PASSES) as i:
                    pool.wait_ge(s_place, i + 1)
                    pool.sem_inc(s_gate, 1)
                    with pool.Fori(0, C) as t:
                        done = i * C + t
                        pool.tensor_copy(put_at[:, :], place_i[:, bass.ds(t, 1)]).then_inc(s_stage, 1)
                        pool.tensor_copy(put_row[:, :].unsqueeze(1), rows[:, bass.ds(t, 1), :]).then_inc(s_stage, 1)
                        pool.wait_ge(s_stage, 2 * done + 2)
                        pool.sem_inc(s_gate, 1)
                        pool.indirect_dma_start(
                            out=rows_dram[:, :], out_offset=bass.IndirectOffsetOnAxis(ap=put_at[:, 0:1], axis=0),
                            in_=put_row[:, :], in_offset=None, bounds_check=limit, oob_is_err=False)\
                            .then_inc(s_put, 16)
                        pool.wait_ge(s_put, 16 * done + 16)
                        pool.sem_inc(s_gate, 1)
                    pool.sem_inc(s_whole, 1)

        @block.vector
        def _(dve):
            V = nc.vector
            dve.wait_ge(s_raw, 16 * loads)
            V.tensor_tensor(late[:, :], raw[:, 1, :], raw[:, 0, :], ALU.is_gt).then_inc(s_late, 1)
            dve.wait_ge(s_late, 1)
            V.tensor_reduce(unsorted[:, :], late[:, :], mybir.AxisListType.X, ALU.add).then_inc(s_late, 1)
            dve.wait_ge(s_sum, 1)
            V.tensor_copy(flag[:, :], ps[:, 0:1]).then_inc(s_flag, 1)
            dve.wait_ge(s_flag, 1)
            out_of_order = dve.value_load(flag[0:1, 0:1], min_val=0, max_val=P * C)
            with dve.If(out_of_order > 0):
                V.memset(zeros[:, :], 0.0)
                for field, kind in enumerate((1, 1, 2, 3)):
                    last = V.tensor_copy(rows[:, :, field], raw[:, kind, :])
                last.then_inc(s_made, 1)
                with dve.Fori(0, PASSES) as i:
                    own = Chain(dve, s_own, i * OWN)
                    dve.wait_ge(s_loaded, 16 * i + 16)
                    own(V.tensor_scalar(digit_i[:, :], rows[:, :, 0], BINS - 1, None, ALU.bitwise_and))
                    own(V.tensor_copy(digit[:, :], digit_i[:, :]))
                    own(V.tensor_scalar(digit_i[:, :], rows[:, :, 0], DIGIT, None, ALU.arith_shift_right))
                    own(V.tensor_copy(rows[:, :, 0], digit_i[:, :]))
                    for b in range(BINS):
                        own(V.tensor_scalar(mask[:, b, :], digit[:, :], float(b), None, ALU.is_equal))
                        own(V.tensor_tensor_scan(run[:, b, :], mask[:, b, :], zeros[:, :], 0.0, ALU.add, ALU.add))
                    V.tensor_copy(total[:, :], run[:, :, C - 1]).then_inc(s_total, 1)
                    dve.wait_ge(s_before, i + 1)
                    own(V.tensor_copy(base[:, 0:2, :], ps[:, 0:2 * BINS].rearrange("p (a b) -> p a b", a=2)))
                    own(V.tensor_tensor_scan(base[:, 2, :], base[:, 1, :], zeros[:, 0:BINS], 0.0, ALU.add, ALU.add))
                    own(V.tensor_tensor(base[:, 2, :], base[:, 2, :], base[:, 1, :], ALU.subtract))
                    own(V.tensor_tensor(base[:, 2, :], base[:, 2, :], base[:, 0, :], ALU.add))
                    own(V.tensor_scalar(base[:, 2, :], base[:, 2, :], 1.0, None, ALU.subtract))
                    own(V.memset(place[:, :], 0.0))
                    for b in range(BINS):
                        own(V.scalar_tensor_tensor(run[:, b, :], run[:, b, :], base[:, 2, b:b + 1], mask[:, b, :],
                                                   ALU.add, ALU.mult))
                        own(V.tensor_tensor(place[:, :], place[:, :], run[:, b, :], ALU.add))
                    own(V.tensor_copy(place_i[:, :], place[:, :]))
                    assert own.n == OWN
                    dve.sem_inc(s_place, 1)
                dve.wait_ge(s_loaded, 16 * (PASSES + 1))
                for kind in (1, 2, 3):
                    last = V.tensor_copy(raw[:, kind, :], rows[:, :, kind])
                last.then_inc(s_split, 1)

        @block.tensor
        def _(pe):
            pe.wait_ge(s_late, 2)
            pe.wait_ge(s_const, 16 * len(k.const_loads))
            nc.tensor.matmul(ps[:, 0:1], k.ones[:, :], unsorted[:, :], start=True, stop=True).then_inc(s_sum, 1)
            pe.wait_ge(s_flag, 1)
            out_of_order = pe.value_load(flag[0:1, 0:1], min_val=0, max_val=P * C)
            with pe.If(out_of_order > 0):
                with pe.Fori(0, PASSES) as i:
                    pe.wait_ge(s_total, i + 1)
                    nc.tensor.matmul(ps[:, 0:BINS], k.below[:, :], total[:, :], start=True, stop=True)
                    nc.tensor.matmul(ps[:, BINS:2 * BINS], k.ones[:, :], total[:, :], start=True,
                                     stop=True).then_inc(s_before, 1)


def edge_tables(nc, k, src, dst, rel):
    E, ET, BT = k.E, k.edges.tiles, k.slots.tiles
    with Ctx(nc, "et", k.whole) as c:
        chunks = -(-ET // P)
        raw = c.sb("raw", [P, 4, chunks, P], I32)
        rawf = c.sb("rawf", [P, 4, chunks, P])
        relf = c.sb("relf", [P, ET])
        high = c.sb("high", [P, ET])
        dsti = c.sb("dsti", [P, 2, ET], I32)
        mask = c.sb("mask", [P, RELS, ET])
        run = c.sb("run", [P, RELS, ET])
        zeros = c.sb("zeros", [P, ET])
        total = c.sb("total", [P, RELS])
        before = c.sb("before", [P, 2 * RELS])
        tiles_i = c.sb("tiles_i", [P, 2, RELS], I32)
        tiles_f = c.sb("tiles_f", [P, RELS])
        tile_end = c.sb("tile_end", [P, RELS])
        base = c.sb("base", [P, RELS])
        slot = c.sb("slot", [P, ET])
        slot_p = c.sb("slot_p", [P, 2, ET], I32)
        tile_rel = c.sb("tile_rel", [P, BT])
        ps = c.ps("ps", [P, 4 * chunks, P])
        ps_count = c.ps("ps_count", [P, 512])
        s_pad, s_rows = c.sem("padded"), c.sem("rows")
        s_rowf, s_turned, s_own = c.sem("row_floats"), c.sem("turned"), c.sem("own")
        s_total, s_before, s_zero = c.sem("totals"), c.sem("before_sem"), c.sem("zero_slots")
        s_back = c.sem("slots_zeroed")
        block = c.block()
        lists = [(src, 0, E), (dst, 0, E), (dst, 1, E - 1), (rel, 0, E)]
        loads = sum((n // P > 0) + (n // P > P) + (n % P > 0) for _, _, n in lists)

        @block.sync
        def _(sp):
            sp.wait_ge(s_pad, 4)
            for kind, (a, first, n) in enumerate(lists):
                full, rest = divmod(n, P)
                for ch in range(chunks):
                    rows = min(full - ch * P, P)
                    if rows > 0:
                        at = first + ch * P * P
                        sp.dma_start(raw[0:rows, kind, ch, :],
                                     a[at:at + rows * P].rearrange("(r i) -> r i", i=P)).then_inc(s_rows, 16)
                if rest:
                    at = first + full * P
                    sp.dma_start(raw[full % P:full % P + 1, kind, full // P, 0:rest],
                                 a[at:at + rest].rearrange("(r i) -> r i", r=1)).then_inc(s_rows, 16)
            sp.wait_ge(s_zero, 1)
            sp.dma_start(k.slot_src_dram.rearrange("(p t) o -> p (t o)", p=P), k.slot_src[:, :]).then_inc(s_back, 16)
            sp.wait_ge(s_back, 16)
            sp.wait_ge(k.s_weights, 16 * len(k.weight_loads))

        @block.gpsimd
        def _(pool):
            for kind, fill in enumerate((0, k.N, k.N, RELS)):
                pool.memset(raw[:, kind, :, :], fill).then_inc(s_pad, 1)
            pool.memset(k.ones_b[:, :], 1.0)
            pool.memset(k.eps[:, :], EPS)
            pool.memset(k.slot_src[:, :], 0).then_inc(s_zero, 1)

        @block.vector
        def _(dve):
            own = Chain(dve, s_own)
            own(nc.vector.memset(zeros[:, :], 0.0))
            dve.wait_ge(s_rows, 16 * loads)
            own(nc.vector.tensor_copy(rawf[:, :, :, :], raw[:, :, :, :]))
            nc.vector.tensor_tensor(rawf[:, 2, :, :], rawf[:, 1, :, :], rawf[:, 2, :, :],
                                    ALU.not_equal).then_inc(s_rowf, 1)
            dve.wait_ge(s_turned, 1)
            for kind, out in ((0, k.src_f), (1, k.dst_f), (2, k.last_f), (3, relf)):
                for ch in range(chunks):
                    w = min(ET - ch * P, P)
                    own(nc.vector.tensor_copy(out[:, ch * P:ch * P + w], ps[:, kind * chunks + ch, 0:w]))
            own(nc.vector.tensor_copy(k.src_i[:, :], k.src_f[:, :]))
            own(nc.vector.tensor_copy(dsti[:, 0, :], k.dst_f[:, :]))
            own(nc.vector.tensor_scalar(dsti[:, 1, :], dsti[:, 0, :], 7, None, ALU.arith_shift_right))
            own(nc.vector.tensor_copy(high[:, :], dsti[:, 1, :]))
            own(nc.vector.tensor_scalar(k.dst_high[:, :], high[:, :], -float(k.node_cols // 2), None, ALU.add))
            own(nc.vector.tensor_scalar(dsti[:, 1, :], dsti[:, 0, :], P - 1, None, ALU.bitwise_and))
            own(nc.vector.tensor_copy(k.dst_low[:, :], dsti[:, 1, :]))
            own(nc.vector.memset(k.dst_before[:, 0:1], -1.0))
            own(nc.vector.tensor_scalar(k.dst_before[:, 1:ET], k.dst_f[:, 0:ET - 1], k.is_last[:, 0:1],
                                        k.is_last[:, 1:2], ALU.mult, ALU.add))
            for r in range(RELS):
                last = nc.vector.tensor_scalar(mask[:, r, :], relf[:, :], float(r), None, ALU.is_equal)
            own(last)
            for r in range(RELS):
                last = nc.vector.tensor_tensor_scan(run[:, r, :], mask[:, r, :], zeros[:, :], 0.0, ALU.add, ALU.add)
            own(last)
            nc.vector.tensor_copy(total[:, :], run[:, :, ET - 1]).then_inc(s_total, 1)
            dve.wait_ge(s_before, 1)
            own(nc.vector.tensor_copy(before[:, :], ps_count[:, 0:2 * RELS]))
            own(nc.vector.tensor_scalar(tiles_f[:, :], before[:, RELS:2 * RELS], float(P - 1), None, ALU.add))
            own(nc.vector.tensor_copy(tiles_i[:, 0, :], tiles_f[:, :]))
            own(nc.vector.tensor_scalar(tiles_i[:, 1, :], tiles_i[:, 0, :], 7, None, ALU.arith_shift_right))
            own(nc.vector.tensor_copy(tiles_f[:, :], tiles_i[:, 1, :]))
            own(nc.vector.tensor_tensor_scan(tile_end[:, :], tiles_f[:, :], zeros[:, 0:RELS], 0.0, ALU.add, ALU.add))
            own(nc.vector.tensor_tensor(tiles_f[:, :], tile_end[:, :], tiles_f[:, :], ALU.subtract))
            own(nc.vector.scalar_tensor_tensor(base[:, :], tiles_f[:, :], float(P), before[:, 0:RELS],
                                               ALU.mult, ALU.add))
            own(nc.vector.tensor_scalar(base[:, :], base[:, :], 1.0, None, ALU.subtract))
            own(nc.vector.tensor_scalar(slot[:, :], relf[:, :], float(RELS), NOWHERE, ALU.is_equal, ALU.mult))
            for r in range(RELS):
                own(nc.vector.scalar_tensor_tensor(run[:, r, :], run[:, r, :], base[:, r:r + 1], mask[:, r, :],
                                                   ALU.add, ALU.mult))
                own(nc.vector.tensor_tensor(slot[:, :], slot[:, :], run[:, r, :], ALU.add))
            own(nc.vector.tensor_copy(k.slot_i[:, :], slot[:, :]))
            own(nc.vector.tensor_scalar(slot_p[:, 0, :], k.slot_i[:, :], P - 1, None, ALU.bitwise_and))
            own(nc.vector.tensor_scalar(slot_p[:, 1, :], k.slot_i[:, :], 7, None, ALU.arith_shift_right))
            own(nc.vector.tensor_copy(mask[:, 0, :], slot_p[:, 0, :]))
            own(nc.vector.tensor_copy(mask[:, 1, :], slot_p[:, 1, :]))
            own(nc.vector.scalar_tensor_tensor(mask[:, 2, :], mask[:, 0, :], float(BT), mask[:, 1, :],
                                               ALU.mult, ALU.add))
            own(nc.vector.tensor_scalar(mask[:, 3, :], slot[:, :], NOWHERE, NOWHERE, ALU.is_ge, ALU.mult))
            own(nc.vector.tensor_tensor(mask[:, 2, :], mask[:, 2, :], mask[:, 3, :], ALU.add))
            own(nc.vector.tensor_copy(k.slot_at[:, :], mask[:, 2, :]))
            own(nc.vector.memset(tile_rel[:, :], 0.0))
            for r in range(RELS - 1):
                own(nc.vector.scalar_tensor_tensor(tile_rel[:, :], k.iota[:, 0:BT], tile_end[:, r:r + 1],
                                                   tile_rel[:, :], ALU.is_ge, ALU.add))
            own(nc.vector.tensor_scalar(tile_rel[:, :], tile_rel[:, :], float(k.D), None, ALU.mult))
            own(nc.vector.tensor_copy(k.tile_weight[:, :], tile_rel[:, :]))

        @block.tensor
        def _(pe):
            pe.wait_ge(s_rowf, 1)
            for kind in range(4):
                for ch in range(chunks):
                    w = min(ET - ch * P, P)
                    last = nc.tensor.transpose(ps[:, kind * chunks + ch, 0:w], rawf[0:w, kind, ch, :],
                                               k.ident[0:w, 0:w])
            last.then_inc(s_turned, 1)
            pe.wait_ge(s_total, 1)
            nc.tensor.matmul(ps_count[:, 0:RELS], k.below[:, :], total[:, :], start=True, stop=True)
            nc.tensor.matmul(ps_count[:, RELS:2 * RELS], k.ones[:, :], total[:, :], start=True,
                             stop=True).then_inc(s_before, 1)


def degree_tables(nc, k):
    ET, NT = k.edges.tiles, k.node_cols
    HOT = 4
    with Ctx(nc, "dt", k.whole) as c:
        hot_low = c.sb("hot_low", [P, HOT, P], BF16)
        hot_high = c.sb("hot_high", [P, HOT, NT], BF16)
        iota_low = c.sb("iota_low", [P, P], BF16)
        iota_high = c.sb("iota_high", [P, NT], BF16)
        hist = c.sb("hist", [P, NT])
        zeros = c.sb("zeros", [P, NT])
        scan = c.sb("scan", [P, NT])
        tmp = c.sb("tmp", [P, 2, NT])
        turned = c.sb("turned", [P, -(-NT // P), P])
        work = c.sb("work", [P, 4, k.D])
        work_b = c.sb("work_b", [P, k.D], BF16)
        ps_hist = c.ps("ps_hist", [P, 512])
        ps_sum = c.ps("ps_sum", [P, 2, 512])
        ps_turn = c.ps("ps_turn", [P, 4, P])
        s_hot, s_counted, s_own = c.sem("hot"), c.sem("counted"), c.sem("own")
        s_hist, s_sums, s_root = c.sem("hist_sem"), c.sem("sums"), c.sem("root")
        s_dinv, s_turn, s_copied, s_out = c.sem("dinv"), c.sem("turn"), c.sem("copied"), c.sem("out")
        slots, early = Scatter(c, k, 0), k.early_groups
        block = c.block()
        def each_tile(eng, step):
            turns = (ET - 1) // HOT - 1
            for t in range(HOT):
                step(t, t)
            with eng.Fori(0, turns) as i:
                for u in range(HOT):
                    step(HOT * i + HOT + u, u)
            for t in range(HOT * (turns + 1), ET):
                step(t, t % HOT)

        def column(table, t):
            return table[:, t:t + 1] if isinstance(t, int) else table[:, bass.ds(t, 1)]

        @block.vector
        def _(dve):
            def step(t, b):
                wait(dve, s_counted, t - HOT + 1)
                nc.vector.tensor_scalar(hot_low[:, b, :], iota_low[:, :], column(k.dst_low, t), None, ALU.is_equal)
                nc.vector.tensor_scalar(hot_high[:, b, :], iota_high[:, :], column(k.dst_high, t), None,
                                        ALU.is_equal).then_inc(s_hot, 1)

            own = Chain(dve, s_own)
            own(nc.vector.tensor_copy(iota_low[:, :], k.iota[:, 0:P]))
            own(nc.vector.tensor_scalar(iota_high[:, :], k.iota[:, 0:NT], -float(NT // 2), None, ALU.add))
            each_tile(dve, step)
            own(nc.vector.memset(zeros[:, :], 0.0))
            dve.wait_ge(s_counted, ET)
            own(nc.vector.tensor_copy(hist[:, :], ps_hist[:, 0:NT]))
            own(nc.vector.tensor_scalar(tmp[:, 0, :], hist[:, :], 1.0, None, ALU.add))
            nc.vector.tensor_scalar(k.has_edge[:, :], hist[:, :], 0.5, None, ALU.is_gt).then_inc(s_hist, 1)
            dve.wait_ge(s_root, 1)
            nc.vector.reciprocal(k.dinv[:, :], tmp[:, 1, :]).then_inc(s_dinv, 1)
            own(nc.vector.reciprocal(k.dinv2[:, :], tmp[:, 0, :]))
            dve.wait_ge(s_dinv, 1)
            own(nc.vector.tensor_tensor(k.sum_gain[:, :], k.has_edge[:, :], k.dinv[:, :], ALU.mult))
            split_row(own, nc, k, k.bias_all[:, :], k.bias_parts[:, :], work, work_b)
            dve.wait_ge(s_sums, 1)
            own(nc.vector.tensor_copy(tmp[:, 0, :], ps_sum[:, 0, 0:NT]))
            own(nc.vector.tensor_tensor_scan(scan[:, :], tmp[:, 0, :], zeros[:, :], 0.0, ALU.add, ALU.add))
            own(nc.vector.tensor_tensor(scan[:, :], scan[:, :], tmp[:, 0, :], ALU.subtract))
            own(nc.vector.tensor_tensor(scan[:, :], scan[:, :], ps_sum[:, 1, 0:NT], ALU.add))
            own(nc.vector.tensor_scalar(hist[:, :], k.has_edge[:, :], -NOWHERE, NOWHERE - 1.0, ALU.mult, ALU.add))
            own(nc.vector.tensor_tensor(scan[:, :], scan[:, :], hist[:, :], ALU.add))
            own(nc.vector.tensor_copy(k.sum_row[:, :], scan[:, :]))
            for ch in range(-(-NT // P)):
                w = min(NT - ch * P, P)
                dve.wait_ge(s_turn, -(-NT // P))
                nc.vector.tensor_copy(turned[0:w, ch, :], ps_turn[0:w, ch, :]).then_inc(s_copied, 1)

        @block.gpsimd
        def _(pool):
            last_slot = pool.to_reg(k.slot_src_dram.shape[0] - 1)
            for g in range(2):
                slots.put(pool, last_slot, g, g, 0)
            if early > 2:
                with pool.Fori(0, early // 2 - 1) as i:
                    for u in range(2):
                        slots.put(pool, last_slot, 2 * i + 2 + u, u, i + 1)
            slots.landed(pool, early)

        @block.scalar
        def _(act):
            act.wait_ge(s_hist, 1)
            nc.scalar.activation(tmp[:, 1, :], tmp[:, 0, :], ACT.Sqrt).then_inc(s_root, 1)

        @block.tensor
        def _(pe):
            def step(t, b):
                pe.wait_ge(s_hot, t + 1)
                nc.tensor.matmul(ps_hist[:, 0:NT], hot_low[:, b, :], hot_high[:, b, :],
                                 start=isinstance(t, int) and t == 0,
                                 stop=isinstance(t, int) and t == ET - 1).then_inc(s_counted, 1)

            each_tile(pe, step)
            pe.wait_ge(s_hist, 1)
            nc.tensor.matmul(ps_sum[:, 0, 0:NT], k.ones[:, :], hist[:, :], start=True, stop=True)
            nc.tensor.matmul(ps_sum[:, 1, 0:NT], k.upto[:, :], hist[:, :], start=True, stop=True).then_inc(s_sums, 1)
            pe.wait_ge(s_dinv, 1)
            for ch in range(-(-NT // P)):
                w = min(NT - ch * P, P)
                nc.tensor.transpose(ps_turn[0:w, ch, :], k.dinv[:, ch * P:ch * P + w],
                                    k.ident[:, :]).then_inc(s_turn, 1)

        @block.sync
        def _(sp):
            n = -(-NT // P)
            for ch in range(n):
                w = min(NT - ch * P, P)
                sp.wait_ge(s_copied, ch + 1)
                sp.dma_start(k.dinv_dram[ch * P * P:ch * P * P + w * P, :].rearrange("(r i) o -> r (i o)", i=P),
                             turned[0:w, ch, :]).then_inc(s_out, 16)
            sp.wait_ge(s_out, 16 * n)


def sum_edges(nc, k, layer, dst):
    plan, D = k.edges, k.D
    first = layer == 0
    W = D if first else 2 * D
    with Ctx(nc, f"se{layer}", k.whole) as c:
        index = c.sb("index", [P, NB, J], I32)
        X = c.sb("X", [P, NB, J, D]) if first else None
        H = c.sb("H", [P, NB, J, D])
        dv = c.sb("dv", [P, NB, J])
        dst_row = c.sb("dst_row", [P, NB, J * P], I32)
        S = c.sb("S", [P, NB, J, P])
        Q = c.sb("Q", [P, NB, J, P])
        T = c.sb("T", [P, NB, J, W])
        bn = c.sb("bn", [P, 2, J, 6])
        mv = c.sb("mv", [P, NB, J, 2])
        small = c.sb("small", [P, NB, 3, J])
        psT = [[c.ps(f"psT{b}{j}", [P, 512]) for j in range(J)] for b in range(2)]
        s_idx, s_gx, s_gd = c.sem("index_sem"), c.pool_sems("rows_in"), c.pool_sems("dinv_in")
        s_dr, s_S, s_zero = c.sems("dst_in"), c.sem("select"), c.sem("zeroed")
        s_var, s_root, s_scale, s_H = c.sem("var"), c.sem("root"), c.sem("scale"), c.sem("normed")
        s_mm, s_T, s_st = c.sem("summed"), c.sem("kept"), c.sems("stored")
        s_sq, s_add = c.sem("squared"), c.sem("added")
        s_own, s_stats, s_gate = c.sem("own"), c.sem("stats"), c.sem("gate")
        block = c.block()
        lo, full = NB + 1, plan.full_groups

        @block.gpsimd
        def _(pool):
            table = k.x_dram if first else k.msg_dram
            limit = pool.to_reg(table.shape[0] - 1)
            nodes = pool.to_reg(k.dinv_dram.shape[0] - 1)

            def step(g):
                if first:
                    wait(pool, s_H, g.number - NB + 1)
                else:
                    wait(pool, s_mm, (g.number - NB + 1) * J)
                pool.wait_ge(s_idx, g.number + 1)
                pool.sem_inc(s_gate, 1)
                for j in range(g.tiles):
                    at = index[0:g.n, g.par, j:j + 1]
                    gather(pool, (X if first else H)[0:g.n, g.par, j, :], table, at, limit)\
                        .then_inc(s_gx[g.par], 16)
                    if first:
                        gather(pool, dv[0:g.n, g.par, j:j + 1], k.dinv_dram, at, nodes)\
                            .then_inc(s_gd[g.par], 16)

            sweep(pool, plan, 0, lo, full, plan.groups, step)

        @block.sync
        def _(sp):
            def step(s):
                g = s.at(4)
                if g.exists:
                    wait(sp, s_S, g.number - NB + 1)
                    n = g.tiles * g.n
                    if isinstance(g.number, int):
                        part = dst[g.number * J * P:g.number * J * P + n]
                    else:
                        part = dst[bass.ds(g.number * (J * P), n)]
                    sp.dma_start(dst_row[:, g.par, 0:n], part.partition_broadcast(P)).then_inc(s_dr[g.par], 16)
                g = s
                if g.exists:
                    sp.wait_ge(s_T, g.tile(g.tiles - 1))
                    sp.dma_start(g.rows(k.sums_dram), T[0:g.n, g.par, 0:g.tiles, 0:D]).then_inc(s_st[g.par], 16)

            sweep(sp, plan, -4, lo, full - 4, plan.groups, step)
            all_stored(sp, s_st, plan)

        @block.vector
        def _(dve):
            if not first:
                nc.vector.memset(k.total[:, :, :], 0.0).then_inc(s_zero, 1)
                dve.wait_ge(s_zero, 1)

            table = k.src_i if first else k.slot_i
            for r in range(NB):
                stage_indices(nc, dve, Group(plan, 0, r), index, table, s_gate, s_idx)

            def step(s):
                if not first and s.at(1).exists:
                    dve.wait_ge(s_gx[s.at(1).par], s.at(1).loads())
                    stage_indices(nc, dve, s.at(1 + NB), index, table, s_gate, s_idx)
                g = s.at(2)
                if g.exists:
                    n, q, w = g.n, g.par, g.tiles
                    wait(dve, s_mm, (g.number - NB + 1) * J)
                    dve.wait_ge(s_dr[q], 16 * g.half + 16)
                    for j in range(w):
                        row = dst_row[:, q, j * P:j * P + n]
                        nc.vector.tensor_scalar(S[0:n, q, j, 0:n], row[0:n, :], g.col(k.dst_f, j), None, ALU.is_equal)
                        last = nc.vector.tensor_scalar(Q[:, q, j, 0:n], row,
                                                       g.col(k.dst_before, j, P), None, ALU.is_equal)
                    last.then_inc(s_S, 1)
                    if first:
                        dve.wait_ge(s_gx[q], g.loads())
                        dve.wait_ge(s_gd[q], g.loads())
                        stage_indices(nc, dve, g.at(NB), index, table, s_gate, s_idx)
                        for j in range(w):
                            last = nc.vector.bn_stats(bn[0:n, g.side, j, :], X[0:n, q, j, :])
                        last.then_inc(s_stats, 1)
                        dve.wait_ge(s_stats, g.number + 1)
                        dve.sem_inc(s_gate, 1)
                        for j in range(w):
                            last = nc.vector.bn_aggr(mv[0:n, q, j, :], bn[0:n, g.side, j, :])
                        last.then_inc(s_var, 1)
                g = s.at(1)
                if g.exists and first:
                    n, q, w = g.n, g.par, g.tiles
                    dve.wait_ge(s_root, g.number + 1)
                    nc.vector.reciprocal(small[0:n, q, 1, 0:w], small[0:n, q, 0, 0:w]).then_inc(s_own, 1)
                    dve.wait_ge(s_own, 2 * g.number + 1)
                    nc.vector.tensor_tensor(small[0:n, q, 1, 0:w], small[0:n, q, 1, 0:w],
                                            dv[0:n, q, 0:w], ALU.mult).then_inc(s_own, 1)
                    dve.wait_ge(s_own, 2 * g.number + 2)
                    nc.vector.scalar_tensor_tensor(small[0:n, q, 2, 0:w], mv[0:n, q, 0:w, 0], -1.0,
                                                   small[0:n, q, 1, 0:w], ALU.mult, ALU.mult).then_inc(s_scale, 1)
                g = s.at(-1)
                if g.exists and not first:
                    n, q = g.n, g.par
                    dve.wait_ge(s_sq, g.number + 1)
                    wait(dve, s_add, g.number)
                    for j in range(g.tiles):
                        last = nc.vector.scalar_tensor_tensor(k.total[0:n, j, :], T[0:n, q, j, :], g.col(k.last_f, j),
                                                              k.total[0:n, j, :], ALU.mult, ALU.add)
                    last.then_inc(s_add, 1)

            sweep(dve, plan, -2, lo, full - 2 - NB, plan.groups + 1, step)

        @block.scalar
        def _(act):
            def step(s):
                g = s
                if g.exists and first:
                    n, q = g.n, g.par
                    act.wait_ge(s_scale, g.number + 1)
                    wait(act, s_mm, (g.number - NB + 1) * J)
                    for j in range(g.tiles):
                        last = nc.scalar.activation(H[0:n, q, j, :], X[0:n, q, j, :], ACT.Relu,
                                                    bias=small[0:n, q, 2, j:j + 1], scale=small[0:n, q, 1, j:j + 1])
                    last.then_inc(s_H, 1)
                g = s.at(-1)
                if g.exists:
                    n, q, w = g.n, g.par, g.tiles
                    wait(act, s_st[q], 16 * g.half)
                    if not first:
                        wait(act, s_add, g.number - NB + 1)
                    for j in range(w):
                        act.wait_ge(s_mm, g.tile(j))
                        last = nc.scalar.activation(T[0:n, q, j, 0:D], psT[g.side][j][0:n, 0:D], ACT.Copy)
                        last.then_inc(s_T, 1)
                    if not first:
                        act.wait_ge(s_T, g.tile(w - 1))
                        nc.scalar.activation(T[0:n, q, 0:w, D:2 * D], T[0:n, q, 0:w, 0:D], ACT.Square).then_inc(s_sq, 1)
                g = s.at(2)
                if g.exists and first:
                    act.wait_ge(s_var, g.number + 1)
                    nc.scalar.activation(small[0:g.n, g.par, 0, 0:g.tiles], mv[0:g.n, g.par, 0:g.tiles, 1],
                                         ACT.Sqrt, bias=k.eps[0:g.n, :]).then_inc(s_root, 1)

            sweep(act, plan, -2, lo, full - 2, plan.groups + 1, step)

        @block.tensor
        def _(pe):
            def own_sum(g, j):
                if j >= g.tiles:
                    return
                if j == 0:
                    if first:
                        pe.wait_ge(s_H, g.number + 1)
                    else:
                        pe.wait_ge(s_gx[g.par], g.loads())
                    pe.wait_ge(s_S, g.number + 1)
                wait(pe, s_T, (g.number - 2) * J + j + 1)
                begin = isinstance(g.number, int) and g.number == 0 and j == 0
                ins = nc.tensor.matmul(psT[g.side][j][0:g.n, 0:D], S[0:g.n, g.par, j, 0:g.n], H[0:g.n, g.par, j, :],
                                       start=True, stop=begin)
                if begin:
                    ins.then_inc(s_mm, 1)

            def step(s):
                for j in range(J):
                    if s.exists and j < s.tiles and not (isinstance(s.number, int) and s.number == 0 and j == 0):
                        q = s.par
                        pe.wait_ge(s_T, s.tile(j) - 1)
                        pq, pj = (q, j - 1) if j else ((q - 1) % NB, J - 1)
                        nc.tensor.matmul(psT[s.side][j][0:s.n, 0:D], Q[:, q, j, 0:s.n], T[:, pq, pj, 0:D],
                                         start=False, stop=True).then_inc(s_mm, 1)
                    if s.at(1).exists:
                        own_sum(s.at(1), j)

            sweep(pe, plan, -1, lo, full - 1, plan.groups, step)


def convolve_nodes(nc, k):
    plan, edges, D = k.nodes, k.edges, k.D
    assert plan.full_groups >= 2 * (edges.full_groups - k.early_groups)
    KC = D // P
    with Ctx(nc, "cn", k.whole) as c:
        index = c.sb("index", [P, NB, J], I32)
        X = c.sb("X", [P, NB, J, D])
        A = c.sb("A", [P, NB, J, D])
        Y = c.sb("Y", [P, NB, J, D])
        YT = c.sb("YT", [P, 2, J * D])
        O = c.sb("O", [P, NB, J, 2 * D])
        bn = c.sb("bn", [P, 2, J, 6])
        mv = c.sb("mv", [P, NB, J, 2])
        small = c.sb("small", [P, NB, 3, J])
        psY = [c.ps(f"psY{b}", [P, 1024]) for b in range(2)]
        psO = [c.ps(f"psO{b}", [P, 1024]) for b in range(2)]
        s_x, s_a, s_idx, s_init = c.sems("x_in"), c.pool_sems("sums_in"), c.sem("index_sem"), c.sem("init")
        s_var, s_root, s_scale, s_relu = c.sem("var"), c.sem("root"), c.sem("scale"), c.sem("relu")
        s_y, s_turn, s_yt, s_mm = c.sem("y"), c.sem("turned"), c.sem("yt"), c.sem("product")
        s_o, s_sq, s_add, s_st = c.sem("o"), c.sem("squared"), c.sem("added"), c.sems("stored")
        s_own, s_stats, s_gate = c.sem("own"), c.sem("stats"), c.sem("gate")
        s_zero, s_got = c.sem("zeroed"), c.sem("slots_in")
        slots, late = Scatter(c, k, k.early_groups), edges.full_groups - k.early_groups
        block = c.block()
        lo, hi, end = NB + 2, plan.full_groups - 3, plan.groups + 2

        def run(eng, start, step):
            sweep(eng, plan, start, lo, hi, end, step)

        @block.sync
        def _(sp):
            def step(s):
                g = s.at(5)
                if g.exists:
                    wait(sp, s_relu, g.number - NB + 1)
                    sp.dma_start(X[0:g.n, g.par, 0:g.tiles, :], g.rows(k.x_dram)).then_inc(s_x[g.par], 16)
                g = s.at(-1)
                if g.exists:
                    sp.wait_ge(s_o, g.number + 1)
                    sp.dma_start(g.rows(k.o_dram), O[0:g.n, g.par, 0:g.tiles, 0:D]).then_inc(s_st[g.par], 16)

            sweep(sp, plan, -5, lo, plan.full_groups - 5, end, step)
            all_stored(sp, s_st, plan)
            slots.landed(sp, late, edges.tail > 0)
            sp.dma_start(k.slot_src[:, :], k.slot_src_dram.rearrange("(p t) o -> p (t o)", p=P)).then_inc(s_got, 16)
            sp.wait_ge(s_got, 16)

        @block.gpsimd
        def _(pool):
            limit = pool.to_reg(k.E - 1)
            last_slot = pool.to_reg(k.slot_src_dram.shape[0] - 1)
            pool.memset(A[:, :, :, :], 0.0).then_inc(s_init, 1)
            pool.wait_ge(s_init, 1)

            def step(s, scatters=True):
                g = s.at(3)
                if g.exists:
                    wait(pool, s_y, g.number - NB + 1)
                    pool.sem_inc(s_gate, 1)
                    pool.tensor_copy(index[0:g.n, g.par, 0:g.tiles], g.cols(k.sum_row)).then_inc(s_idx, 1)
                    pool.wait_ge(s_idx, g.number + 1)
                    pool.sem_inc(s_gate, 1)
                    for j in range(g.tiles):
                        gather(pool, A[0:g.n, g.par, j, :], k.sums_dram, index[0:g.n, g.par, j:j + 1], limit)\
                            .then_inc(s_a[g.par], 16)
                if scatters and s.r % 2 == 0 and s.r >= 0:
                    group = s.loop * (NB // 2) + s.r // 2
                    if not isinstance(group, int) or group < late:
                        slots.put(pool, last_slot, group, (s.r // 2) % 2, s.half)

            spent = 2 * late
            turn = lo + max(0, (min(spent, hi) - lo) // NB) * NB
            sweep(pool, plan, -3, lo, turn, turn, step)
            sweep(pool, plan, turn, max(turn, spent), hi, end,
                  lambda s: step(s, isinstance(s.loop, int)))
            if edges.tail:
                slots.put(pool, last_slot, late, late % 2, late // 2, 1)

        @block.vector
        def _(dve):
            nc.vector.memset(k.total[:, :, :], 0.0).then_inc(s_zero, 1)
            dve.wait_ge(s_zero, 1)

            def step(s):
                g, f = s.at(2), s.at(3)
                n, q, w = g.n, g.par, g.tiles
                if g.exists:
                    dve.wait_ge(s_root, g.number + 1)
                    nc.vector.reciprocal(small[0:n, q, 1, 0:w], small[0:n, q, 0, 0:w]).then_inc(s_own, 1)
                if f.exists:
                    dve.wait_ge(s_x[f.par], 16 * f.half + 16)
                    for j in range(f.tiles):
                        last = nc.vector.bn_stats(bn[0:f.n, f.side, j, :], X[0:f.n, f.par, j, :])
                    last.then_inc(s_stats, 1)
                if g.exists:
                    dve.wait_ge(s_own, 2 * g.number + 1)
                    nc.vector.tensor_tensor(small[0:n, q, 1, 0:w], small[0:n, q, 1, 0:w], g.cols(k.dinv2),
                                            ALU.mult).then_inc(s_own, 1)
                if f.exists:
                    dve.wait_ge(s_stats, f.number + 1)
                    dve.sem_inc(s_gate, 1)
                    for j in range(f.tiles):
                        last = nc.vector.bn_aggr(mv[0:f.n, f.par, j, :], bn[0:f.n, f.side, j, :])
                    last.then_inc(s_var, 1)
                if g.exists:
                    dve.wait_ge(s_own, 2 * g.number + 2)
                    nc.vector.scalar_tensor_tensor(small[0:n, q, 2, 0:w], mv[0:n, q, 0:w, 0], -1.0,
                                                   small[0:n, q, 1, 0:w], ALU.mult, ALU.mult).then_inc(s_scale, 1)
                g = s.at(1)
                if g.exists:
                    n, q = g.n, g.par
                    dve.wait_ge(s_relu, g.number + 1)
                    dve.wait_ge(s_a[q], g.loads())
                    for j in range(g.tiles):
                        last = nc.vector.scalar_tensor_tensor(Y[0:n, q, j, :], A[0:n, q, j, :], g.col(k.sum_gain, j),
                                                              Y[0:n, q, j, :], ALU.mult, ALU.add)
                    last.then_inc(s_y, 1)
                g = s.at(-2)
                if g.exists:
                    n, q, w = g.n, g.par, g.tiles
                    dve.wait_ge(s_sq, g.number + 1)
                    wait(dve, s_add, g.number)
                    nc.vector.tensor_tensor(k.total[0:n, 0:w, :], O[0:n, q, 0:w, :], k.total[0:n, 0:w, :],
                                            ALU.add).then_inc(s_add, 1)

            run(dve, -3, step)

        @block.scalar
        def _(act):
            def step(s):
                g = s
                if g.exists:
                    act.wait_ge(s_turn, g.number + 1)
                    wait(act, s_mm, g.number - 1)
                    c = g.tiles * KC
                    nc.scalar.activation(YT[:, g.side, 0:c * P].rearrange("p (c n) -> p c n", c=c)[:, :, 0:g.n],
                                         psY[g.side][:, 0:c * P].rearrange("p (c n) -> p c n", c=c)[:, :, 0:g.n],
                                         ACT.Copy).then_inc(s_yt, 1)
                g = s.at(2)
                if g.exists:
                    n, q = g.n, g.par
                    act.wait_ge(s_scale, g.number + 1)
                    wait(act, s_turn, g.number - NB + 1)
                    for j in range(g.tiles):
                        last = nc.scalar.activation(Y[0:n, q, j, :], X[0:n, q, j, :], ACT.Relu,
                                                    bias=small[0:n, q, 2, j:j + 1], scale=small[0:n, q, 1, j:j + 1])
                    last.then_inc(s_relu, 1)
                g = s.at(3)
                if g.exists:
                    act.wait_ge(s_var, g.number + 1)
                    nc.scalar.activation(small[0:g.n, g.par, 0, 0:g.tiles], mv[0:g.n, g.par, 0:g.tiles, 1],
                                         ACT.Sqrt, bias=k.eps[0:g.n, :]).then_inc(s_root, 1)
                g = s.at(-1)
                if g.exists:
                    n, q, w = g.n, g.par, g.tiles
                    act.wait_ge(s_mm, g.number + 1)
                    wait(act, s_add, g.number - NB + 1)
                    wait(act, s_st[q], 16 * g.half)
                    nc.scalar.activation(O[0:n, q, 0:w, 0:D],
                                         psO[g.side][0:n, 0:w * D].rearrange("p (j d) -> p j d", d=D),
                                         ACT.Copy).then_inc(s_o, 1)
                    act.wait_ge(s_o, g.number + 1)
                    nc.scalar.activation(O[0:n, q, 0:w, D:2 * D], O[0:n, q, 0:w, 0:D], ACT.Square).then_inc(s_sq, 1)

            run(act, -3, step)

        @block.tensor
        def _(pe):
            def step(s):
                g = s
                if g.exists:
                    n, q = g.n, g.par
                    pe.wait_ge(s_y, g.number + 1)
                    wait(pe, s_yt, g.number - 1)
                    for j in range(g.tiles):
                        for kc in range(KC):
                            at = (j * KC + kc) * P
                            last = nc.tensor.transpose(psY[g.side][:, at:at + n], Y[0:n, q, j, kc * P:(kc + 1) * P],
                                                       k.ident[0:n, 0:n])
                    last.then_inc(s_turn, 1)
                g = s.at(-1)
                if g.exists:
                    n = g.n
                    pe.wait_ge(s_yt, g.number + 1)
                    wait(pe, s_o, g.number - 1)
                    for j in range(g.tiles):
                        out = psO[g.side][0:n, j * D:(j + 1) * D]
                        nc.tensor.matmul(out, k.ones_b[:, 0:n], k.bias_parts[:, :], start=True, stop=False)
                        for kc in range(KC):
                            at = (j * KC + kc) * P
                            last = nc.tensor.matmul(out, YT[:, g.side, at:at + n], k.w0[:, kc, :],
                                                    start=False, stop=kc == KC - 1)
                    last.then_inc(s_mm, 1)

            run(pe, -2, step)


def split_row(dve_own, nc, k, row, parts, work, work_b):
    V, own = nc.vector, dve_own
    own(V.tensor_copy(work[:, 0, :], row))
    for i in range(3):
        own(V.tensor_copy(work_b[:, :], work[:, 0, :]))
        own(V.tensor_copy(work[:, 1 + i, :], work_b[:, :]))
        own(V.tensor_tensor(work[:, 0, :], work[:, 0, :], work[:, 1 + i, :], ALU.subtract))
    own(V.tensor_scalar(work[:, 1, :], work[:, 1, :], k.ident[:, 0:1], None, ALU.mult))
    own(V.scalar_tensor_tensor(work[:, 1, :], work[:, 2, :], k.ident[:, 1:2], work[:, 1, :], ALU.mult, ALU.add))
    own(V.scalar_tensor_tensor(work[:, 1, :], work[:, 3, :], k.ident[:, 2:3], work[:, 1, :], ALU.mult, ALU.add))
    own(V.tensor_copy(parts, work[:, 1, :]))


def column_norm(nc, k, layer, gamma, beta, coef):
    D, N = k.D, k.N
    with Ctx(nc, f"bc{layer}", k.whole) as c:
        gb = c.sb("gb", [1, 2, D])
        stat = c.sb("stat", [1, 2 * D])
        row = c.sb("row", [1, 2 * D])
        t = c.sb("t", [1, 3, D])
        work = c.sb("work", [P, 4, D])
        work_b = c.sb("work_b", [P, D], BF16)
        ps = c.ps("ps", [P, 512])
        ps_stat = c.ps("ps_stat", [P, 512])
        s_in, s_sum, s_own, s_var, s_root, s_row, s_all = [
            c.sem(n) for n in ("in", "sum", "own", "var", "root", "row_sem", "all")]
        block = c.block()

        @block.sync
        def _(sp):
            sp.dma_start(gb[0:1, 0, :], gamma.rearrange("(a d) -> a d", a=1)).then_inc(s_in, 16)
            sp.dma_start(gb[0:1, 1, :], beta.rearrange("(a d) -> a d", a=1)).then_inc(s_in, 16)

        @block.vector
        def _(dve):
            own = Chain(dve, s_own)
            dve.wait_ge(s_sum, 1)
            own(nc.vector.tensor_scalar(stat[:, :], ps_stat[0:1, 0:2 * D], 1.0 / N, None, ALU.mult))
            own(nc.vector.tensor_tensor(t[:, 0, :], stat[:, 0:D], stat[:, 0:D], ALU.mult))
            own(nc.vector.tensor_tensor(t[:, 0, :], stat[:, D:2 * D], t[:, 0, :], ALU.subtract))
            nc.vector.tensor_scalar(t[:, 0, :], t[:, 0, :], 0.0, EPS, ALU.max, ALU.add).then_inc(s_var, 1)
            dve.wait_ge(s_root, 1)
            own(nc.vector.reciprocal(t[:, 2, :], t[:, 1, :]))
            dve.wait_ge(s_in, 32)
            own(nc.vector.tensor_tensor(row[:, 0:D], t[:, 2, :], gb[0:1, 0, :], ALU.mult))
            own(nc.vector.tensor_tensor(t[:, 0, :], row[:, 0:D], stat[:, 0:D], ALU.mult))
            nc.vector.tensor_tensor(row[:, D:2 * D], gb[0:1, 1, :], t[:, 0, :], ALU.subtract).then_inc(s_row, 1)
            dve.wait_ge(s_all, 1)
            own(nc.vector.tensor_copy(coef[:, :], ps[:, 0:2 * D]))
            if layer:
                split_row(own, nc, k, coef[:, D:2 * D], k.shift_parts[:, :], work, work_b)

        @block.scalar
        def _(act):
            act.wait_ge(s_var, 1)
            nc.scalar.activation(t[:, 1, :], t[:, 0, :], ACT.Sqrt).then_inc(s_root, 1)

        @block.tensor
        def _(pe):
            for j in range(J):
                last = nc.tensor.matmul(ps_stat[0:1, 0:2 * D], k.ones[:, 0:1], k.total[:, j, :],
                                        start=j == 0, stop=j == J - 1)
            last.then_inc(s_sum, 1)
            pe.wait_ge(s_row, 1)
            nc.tensor.matmul(ps[:, 0:2 * D], k.ones[0:1, :], row[0:1, :], start=True, stop=True).then_inc(s_all, 1)


def relate_messages(nc, k):
    plan, D = k.slots, k.D
    KC = D // P
    NEWTON = 3
    OWN = 3 + 3 * NEWTON
    with Ctx(nc, "rm", k.whole) as c:
        index = c.sb("index", [P, NB, J], I32)
        X = c.sb("X", [P, NB, J, D])
        O = c.sb("O", [P, NB, J, D])
        H = c.sb("H", [P, 2, J, D])
        HT = c.sb("HT", [P, 2, J * D])
        M = c.sb("M", [P, NB, J, D])
        bn = c.sb("bn", [P, 2, J, 6])
        mv = c.sb("mv", [P, 2, J, 2])
        root = c.sb("root", [P, 4, J])
        guess = c.sb("guess", [P, 2, J], I32)
        small = c.sb("small", [P, NB, 2, J])
        psH = [c.ps(f"psH{b}", [P, 1024]) for b in range(2)]
        psM = [c.ps(f"psM{b}", [P, 1024]) for b in range(2)]
        s_x, s_ob = c.pool_sems("x_in"), c.pool_sems("o_in")
        s_idx, s_gate, s_own = c.sem("index_sem"), c.sem("gate"), c.sem("own")
        s_scaled, s_z, s_th, s_scale, s_relu = c.sem("scaled"), c.sem("z"), c.sem("tanh"), c.sem("scale"), c.sem("relu")
        s_x1, s_stats, s_mean = c.sem("x1"), c.sem("stats"), c.sem("mean")
        s_turn, s_ht, s_mm, s_m, s_st = c.sem("turned"), c.sem("ht"), c.sem("product"), c.sem("m"), c.sems("stored")
        block = c.block()
        lo, hi, end = NB + 2, plan.full_groups - 2, plan.groups + 2

        def run(eng, start, step):
            sweep(eng, plan, start, lo, hi, end, step)

        @block.gpsimd
        def _(pool):
            limit = pool.to_reg(k.N - 1)

            def step(g):
                wait(pool, s_x1, g.number - NB + 1)
                pool.wait_ge(s_idx, g.number + 1)
                pool.sem_inc(s_gate, 1)
                for j in range(J):
                    gather(pool, O[:, g.par, j, :], k.o_dram, index[:, g.par, j:j + 1], limit)\
                        .then_inc(s_ob[g.par], 16)
                wait(pool, s_relu, g.number - NB + 1)
                pool.sem_inc(s_gate, 1)
                for j in range(J):
                    gather(pool, X[:, g.par, j, :], k.x_dram, index[:, g.par, j:j + 1], limit)\
                        .then_inc(s_x[g.par], 16)

            sweep(pool, plan, 0, lo, plan.groups, plan.groups, step)

        @block.sync
        def _(sp):
            def step(g):
                sp.wait_ge(s_m, g.number + 1)
                sp.dma_start(g.rows(k.msg_dram), M[:, g.par, :, :]).then_inc(s_st[g.par], 16)

            sweep(sp, plan, 0, lo, plan.groups, plan.groups, step)
            all_stored(sp, s_st, plan)

        @block.vector
        def _(dve):
            V = nc.vector

            for r in range(NB):
                stage_indices(nc, dve, Group(plan, 0, r), index, k.slot_src, s_gate, s_idx)

            def step(s):
                g, f, z = s, s.at(1), s.at(2)

                def scale_o():
                    if z.exists:
                        dve.wait_ge(s_ob[z.par], z.loads())
                        V.tensor_tensor(O[:, z.par, :, :], O[:, z.par, :, :],
                                        k.coef0[:, 0:D].unsqueeze(1).broadcast_to([P, J, D]), ALU.mult)\
                            .then_inc(s_scaled, 1)

                def shift_o():
                    if z.exists:
                        dve.wait_ge(s_scaled, z.number + 1)
                        V.tensor_tensor(O[:, z.par, :, :], O[:, z.par, :, :],
                                        k.coef0[:, D:2 * D].unsqueeze(1).broadcast_to([P, J, D]), ALU.add)\
                            .then_inc(s_z, 1)

                def add_x():
                    if f.exists:
                        dve.wait_ge(s_th, f.number + 1)
                        dve.wait_ge(s_x[f.par], f.loads())
                        stage_indices(nc, dve, f.at(NB), index, k.slot_src, s_gate, s_idx)
                        V.tensor_tensor(X[:, f.par, :, :], X[:, f.par, :, :], O[:, f.par, :, :],
                                        ALU.add).then_inc(s_x1, 1)

                def stats(j):
                    if f.exists:
                        if j == 0:
                            dve.wait_ge(s_x1, f.number + 1)
                        V.bn_stats(bn[:, f.side, j, :], X[:, f.par, j, :]).then_inc(s_stats, 1)

                def means(j):
                    if f.exists:
                        if j == 0:
                            dve.wait_ge(s_stats, f.tile(J - 1))
                            dve.sem_inc(s_gate, 1)
                        V.bn_aggr(mv[:, f.side, j, :], bn[:, f.side, j, :]).then_inc(s_mean, 1)

                def result(n, make):
                    if g.exists:
                        if n > 1:
                            dve.wait_ge(s_own, g.number * OWN + (n - 1))
                        make().then_inc(s_own, 1)

                v, t = root[:, 0, :], root[:, 2, :]
                if g.exists:
                    dve.wait_ge(s_mean, g.tile(J - 1))
                result(1, lambda: V.tensor_scalar(v, mv[:, g.side, :, 1], EPS, None, ALU.add))
                scale_o()
                result(2, lambda: V.tensor_scalar(guess[:, 0, :], v.bitcast(I32), 1, None, ALU.arith_shift_right))
                add_x()
                result(3, lambda: V.tensor_scalar(guess[:, 1, :], guess[:, 0, :], -1.0, float(0x5F3759DF),
                                                  ALU.mult, ALU.add))
                shift_o()
                y = guess[:, 1, :].bitcast(F32)
                for it in range(NEWTON):
                    n = 3 + 3 * it
                    better = small[:, g.par, 0, :] if it == NEWTON - 1 else root[:, 1 + 2 * (it % 2), :]
                    result(n + 1, lambda: V.scalar_tensor_tensor(t, y, -0.5, y, ALU.mult, ALU.mult))
                    if it < 2:
                        (stats, means)[it](0)
                    result(n + 2, lambda: V.tensor_tensor(t, t, v, ALU.mult))
                    if it < 2:
                        (stats, means)[it](1)
                    result(n + 3, lambda: V.scalar_tensor_tensor(better, t, 1.5, y, ALU.add, ALU.mult))
                    if it < 2:
                        (stats, means)[it](2)
                    y = better
                if g.exists:
                    dve.wait_ge(s_own, g.number * OWN + OWN)
                    V.scalar_tensor_tensor(small[:, g.par, 1, :], mv[:, g.side, :, 0], -1.0, small[:, g.par, 0, :],
                                           ALU.mult, ALU.mult).then_inc(s_scale, 1)

            sweep(dve, plan, -2, lo, plan.full_groups - 1 - NB, end, step)

        @block.scalar
        def _(act):
            def step(s):
                g = s.at(-1)
                if g.exists:
                    act.wait_ge(s_turn, g.number + 1)
                    wait(act, s_mm, g.number - 1)
                    nc.scalar.activation(HT[:, g.side, :], psH[g.side][:, 0:J * D], ACT.Copy).then_inc(s_ht, 1)
                g = s.at(2)
                if g.exists:
                    act.wait_ge(s_z, g.number + 1)
                    nc.scalar.activation(O[:, g.par, :, :], O[:, g.par, :, :], ACT.Tanh).then_inc(s_th, 1)
                g = s
                if g.exists:
                    q = g.par
                    act.wait_ge(s_scale, g.number + 1)
                    wait(act, s_turn, g.number - 1)
                    for j in range(J):
                        last = nc.scalar.activation(H[:, g.side, j, :], X[:, q, j, :], ACT.Relu,
                                                    bias=small[:, q, 1, j:j + 1], scale=small[:, q, 0, j:j + 1])
                    last.then_inc(s_relu, 1)
                g = s.at(-2)
                if g.exists:
                    act.wait_ge(s_mm, g.number + 1)
                    wait(act, s_st[g.par], 16 * g.half)
                    nc.scalar.activation(M[:, g.par, :, :],
                                         psM[g.side][:, 0:J * D].rearrange("p (j d) -> p j d", d=D),
                                         ACT.Copy).then_inc(s_m, 1)

            run(act, -2, step)

        @block.tensor
        def _(pe):
            def step(s):
                g = s.at(-1)
                if g.exists:
                    pe.wait_ge(s_ht, g.number + 1)
                    wait(pe, s_m, g.number - 1)
                    for j in range(J):
                        col = g.number * J + j
                        off = pe.value_load(k.tile_weight[0:1, col:col + 1] if isinstance(col, int)
                                            else k.tile_weight[0:1, bass.ds(col, 1)], min_val=0,
                                            max_val=(RELS - 1) * D)
                        for kc in range(KC):
                            at = (j * KC + kc) * P
                            last = nc.tensor.matmul(psM[g.side][:, j * D:(j + 1) * D], HT[:, g.side, at:at + P],
                                                    k.w1[:, kc, bass.ds(off, D)], start=kc == 0, stop=kc == KC - 1)
                    last.then_inc(s_mm, 1)
                g = s
                if g.exists:
                    pe.wait_ge(s_relu, g.number + 1)
                    wait(pe, s_ht, g.number - 1)
                    for j in range(J):
                        for kc in range(KC):
                            at = (j * KC + kc) * P
                            last = nc.tensor.transpose(psH[g.side][:, at:at + P],
                                                       H[:, g.side, j, kc * P:(kc + 1) * P], k.ident[:, :])
                    last.then_inc(s_turn, 1)

            run(pe, 0, step)


def finish_nodes(nc, k, out):
    plan, D = k.nodes, k.D
    with Ctx(nc, "fn", k.whole) as c:
        index = c.sb("index", [P, NB, J], I32)
        X = c.sb("X", [P, NB, J, D])
        Z = c.sb("Z", [P, NB, J, D])
        A = c.sb("A", [P, NB, J, D])
        R = c.sb("R", [P, NB, J, D])
        psR = [c.ps(f"psR{b}", [P, 1024]) for b in range(2)]
        s_x, s_ob, s_a, s_st = c.sems("x_in"), c.sems("o_in"), c.pool_sems("sums_in"), c.sems("stored")
        s_idx, s_init, s_gate, s_own = c.sem("index_sem"), c.sem("init"), c.sem("gate"), c.sem("own")
        s_z, s_th, s_u, s_mm, s_r = c.sem("z"), c.sem("tanh"), c.sem("scaled"), c.sem("summed"), c.sem("result")
        block = c.block()
        lo, hi, end = NB + 1, plan.full_groups - 3, plan.groups + 1

        def run(eng, start, step):
            sweep(eng, plan, start, lo, hi, end, step)

        @block.sync
        def _(sp):
            def step(s):
                g = s.at(3)
                if g.exists:
                    wait(sp, s_mm, g.number - NB + 1)
                    sp.dma_start(Z[0:g.n, g.par, 0:g.tiles, :], g.rows(k.o_dram)).then_inc(s_ob[g.par], 16)
                g = s.at(2)
                if g.exists:
                    wait(sp, s_r, g.number - NB + 1)
                    sp.dma_start(X[0:g.n, g.par, 0:g.tiles, :], g.rows(k.x_dram)).then_inc(s_x[g.par], 16)
                g = s.at(-1)
                if g.exists:
                    sp.wait_ge(s_r, g.number + 1)
                    sp.dma_start(g.rows(out), R[0:g.n, g.par, 0:g.tiles, :]).then_inc(s_st[g.par], 16)

            run(sp, -3, step)
            all_stored(sp, s_st, plan)

        @block.gpsimd
        def _(pool):
            limit = pool.to_reg(k.E - 1)
            pool.memset(A[:, :, :, :], 0.0).then_inc(s_init, 1)
            pool.wait_ge(s_init, 1)

            def step(s):
                g = s.at(3)
                if not g.exists:
                    return
                wait(pool, s_mm, g.number - NB + 1)
                pool.sem_inc(s_gate, 1)
                pool.tensor_copy(index[0:g.n, g.par, 0:g.tiles], g.cols(k.sum_row)).then_inc(s_idx, 1)
                pool.wait_ge(s_idx, g.number + 1)
                pool.sem_inc(s_gate, 1)
                for j in range(g.tiles):
                    gather(pool, A[0:g.n, g.par, j, :], k.sums_dram, index[0:g.n, g.par, j:j + 1], limit)\
                        .then_inc(s_a[g.par], 16)

            run(pool, -3, step)

        @block.vector
        def _(dve):
            def step(s):
                g = s.at(1)
                if g.exists:
                    n, q, w = g.n, g.par, g.tiles
                    dve.wait_ge(s_ob[q], 16 * g.half + 16)
                    nc.vector.tensor_tensor(Z[0:n, q, 0:w, :], Z[0:n, q, 0:w, :],
                                            k.coef0[0:n, 0:D].unsqueeze(1).broadcast_to([n, w, D]), ALU.mult)\
                        .then_inc(s_own, 1)
                    dve.wait_ge(s_own, g.number + 1)
                    nc.vector.tensor_tensor(Z[0:n, q, 0:w, :], Z[0:n, q, 0:w, :],
                                            k.coef0[0:n, D:2 * D].unsqueeze(1).broadcast_to([n, w, D]), ALU.add)\
                        .then_inc(s_z, 1)
                    dve.wait_ge(s_a[q], g.loads())
                    for j in range(w):
                        last = nc.vector.scalar_tensor_tensor(A[0:n, q, j, :], A[0:n, q, j, :], g.col(k.has_edge, j),
                                                              k.coef1[0:n, 0:D], ALU.mult, ALU.mult)
                    last.then_inc(s_u, 1)
                g = s.at(-1)
                if g.exists:
                    n, q, w = g.n, g.par, g.tiles
                    dve.wait_ge(s_x[q], 16 * g.half + 16)
                    wait(dve, s_st[q], 16 * g.half)
                    dve.wait_ge(s_mm, g.number + 1)
                    nc.vector.tensor_tensor(R[0:n, q, 0:w, :],
                                            psR[g.side][0:n, 0:w * D].rearrange("p (j d) -> p j d", d=D),
                                            X[0:n, q, 0:w, :], ALU.add).then_inc(s_r, 1)

            run(dve, -1, step)

        @block.scalar
        def _(act):
            def step(s):
                g = s.at(1)
                if g.exists:
                    act.wait_ge(s_z, g.number + 1)
                    nc.scalar.activation(Z[0:g.n, g.par, 0:g.tiles, :], Z[0:g.n, g.par, 0:g.tiles, :],
                                         ACT.Tanh).then_inc(s_th, 1)

            run(act, -1, step)

        @block.tensor
        def _(pe):
            def step(g):
                if not g.exists:
                    return
                n, q = g.n, g.par
                pe.wait_ge(s_th, g.number + 1)
                pe.wait_ge(s_u, g.number + 1)
                wait(pe, s_r, g.number - 1)
                for j in range(g.tiles):
                    at = psR[g.side][0:n, j * D:(j + 1) * D]
                    nc.tensor.matmul(at, k.ones_b[:, 0:n], k.shift_parts[:, :], start=True, stop=False)
                    nc.tensor.matmul(at, k.ident[0:n, 0:n], Z[0:n, q, j, :], start=False, stop=False)
                    last = nc.tensor.matmul(at, k.ident[0:n, 0:n], A[0:n, q, j, :], start=False, stop=True)
                last.then_inc(s_mm, 1)

            run(pe, 0, step)


class Names:
    pass


def build(nc, x, src, dst, rel, w0, b0, g0, be0, w1, g1, be1, consts, out):
    k = Names()
    k.N, k.D = x.shape
    k.E = src.shape[0]
    D = k.D
    k.nodes, k.edges = Plan(k.N), Plan(k.E)
    slot_tiles = (k.E + RELS * (P - 1)) // P
    slot_tiles = -(-slot_tiles // J) * J
    k.slots = Plan(slot_tiles * P)
    k.node_cols = k.N // P + 1
    ET, BT, NT = k.edges.tiles, k.slots.tiles, k.node_cols
    k.early_groups = 2 * (k.edges.full_groups // EARLY)
    k.x_dram = x
    dram = lambda name, shape, dt: nc.dram_tensor(name, shape, dt, kind="Internal").ap()
    k.src_list, k.dst_list, k.rel_list = (dram(n, (k.E,), I32) for n in ("src_list", "dst_list", "rel_list"))
    k.slot_src_dram = dram("slot_src_dram", (P * BT, 1), I32)
    k.dinv_dram = dram("dinv_dram", (NT * P, 1), F32)
    k.sums_dram = dram("sums_dram", (k.E, D), F32)
    k.o_dram = dram("o_dram", (k.N, D), F32)
    k.msg_dram = dram("msg_dram", (BT * P, D), F32)
    with Ctx(nc, "k") as c:
        k.whole = c
        k.s_weights = c.sem("weights")
        k.ident, k.ones, k.below, k.upto = (c.sb(n, [P, P]) for n in ("ident", "ones", "below", "upto"))
        k.iota = c.sb("iota", [P, 512])
        k.eps = c.sb("eps", [P, 1])
        k.is_last = c.sb("is_last", [P, 2])
        k.w0 = c.sb("w0", [P, D // P, D])
        k.w1 = c.sb("w1", [P, D // P, RELS * D])
        k.bias_all = c.sb("bias_all", [P, D])
        k.src_f, k.dst_f, k.last_f, k.dst_high, k.dst_low, k.dst_before = (
            c.sb(n, [P, ET]) for n in ("src_f", "dst_f", "last_f", "dst_high", "dst_low", "dst_before"))
        k.src_i, k.slot_i, k.slot_at = (c.sb(n, [P, ET], I32) for n in ("src_i", "slot_i", "slot_at"))
        k.slot_src, k.tile_weight = (c.sb(n, [P, BT], I32) for n in ("slot_src", "tile_weight"))
        k.dinv, k.dinv2, k.has_edge, k.sum_gain = (
            c.sb(n, [P, NT]) for n in ("dinv_t", "dinv2", "has_edge", "sum_gain"))
        k.bias_parts = c.sb("bias_parts", [P, D], BF16)
        k.shift_parts = c.sb("shift_parts", [P, D], BF16)
        k.ones_b = c.sb("ones_b", [P, P], BF16)
        k.total = c.sb("total_rows", [P, J, 2 * D])
        k.sum_row = c.sb("sum_row", [P, NT], I32)
        k.coef0, k.coef1 = c.sb("coef0", [P, 2 * D]), c.sb("coef1", [P, 2 * D])
        k.const_loads = [
            (consts[0], k.ident[:, :]), (consts[1], k.ones[:, :]), (consts[2], k.below[:, :]),
            (consts[3], k.upto[:, :]), (consts[4], k.iota[:, :]), (consts[5], k.is_last[:, :])]
        k.weight_loads = [
            (w0.rearrange("(c p) o -> p c o", p=P), k.w0[:, :, :]),
            (b0.partition_broadcast(P), k.bias_all[:, :])]
        k.weight_loads += [(w1[r].rearrange("(c p) o -> p c o", p=P), k.w1[:, :, r * D:(r + 1) * D])
                           for r in range(RELS)]
        order_edges(nc, k, src, dst, rel)
        edge_tables(nc, k, k.src_list, k.dst_list, k.rel_list)
        degree_tables(nc, k)
        sum_edges(nc, k, 0, k.dst_list)
        convolve_nodes(nc, k)
        column_norm(nc, k, 0, g0, be0, k.coef0)
        relate_messages(nc, k)
        sum_edges(nc, k, 1, k.dst_list)
        column_norm(nc, k, 1, g1, be1, k.coef1)
        finish_nodes(nc, k, out)


_INS = ['x', 'src', 'dst', 'edge_type_8', 'L0_gnn_W', 'L0_gnn_b', 'L0_gnn_gamma', 'L0_gnn_beta',
        'L1_gnn_weight', 'L1_gnn_gamma', 'L1_gnn_beta']


def kernel(**inputs):
    import numpy as _np
    import concourse.bacc as _bacc
    from concourse import mybir as _mybir
    from concourse.bass_utils import run_bass_kernel_spmd as _run

    nc = _bacc.Bacc("TRN2", target_bir_lowering=False, num_devices=1)
    arrays, args = {}, []

    def given(name, a):
        arrays[name] = a
        return nc.dram_tensor(name, a.shape, _mybir.dt.from_np(a.dtype), kind="ExternalInput").ap()

    for name in _INS:
        args.append(given(f"in_{name}_dram", _np.ascontiguousarray(inputs[name])))
    n = _np.arange(P)
    last = (n == P - 1).astype(_np.float32)
    shapes_only = [
        _np.eye(P, dtype=_np.float32), _np.ones((P, P), _np.float32),
        (n[:, None] < n[None, :]).astype(_np.float32), (n[:, None] <= n[None, :]).astype(_np.float32),
        _np.tile(_np.arange(512, dtype=_np.float32), (P, 1)), _np.stack([last, last - 1], 1)]
    args.append([given(f"const_{i}_dram", _np.ascontiguousarray(a)) for i, a in enumerate(shapes_only)])
    shape = inputs['x'].shape
    args.append(nc.dram_tensor("out_0_dram", shape, _mybir.dt.float32, kind="ExternalOutput").ap())
    build(nc, *args)
    r = _run(nc, [arrays], core_ids=[0])
    return r.results[0]["out_0_dram"]
```
